# Optimizing a Trainium2 kernel written in Bass

```python
import numpy as np
import jax
import jax.numpy as jnp

def _softmax(x, axis=-1):
    return jax.nn.softmax(x, axis=axis)

def _gelu(x):
    return jax.nn.gelu(x, approximate=True)

def _silu(x):
    return jax.nn.silu(x)

def _sigmoid(x):
    return jax.nn.sigmoid(x)

def _layernorm(x, axis=-1, eps=1e-05):
    m = jnp.mean(x, axis=axis, keepdims=True)
    v = jnp.var(x, axis=axis, keepdims=True)
    return (x - m) / jnp.sqrt(v + eps)

def _scatter_add(tgt, idx, src, axis=0):
    return tgt.at[idx].add(src)

def _segment_sum(src, seg, n):
    return jax.ops.segment_sum(src, seg, n)
kernel_name = 'mk_xattn_ffn_d1_seqx_r8_ba46fb'

def setup_inputs(seed: int=0):
    np.random.seed(seed)
    _w = jnp.asarray

    def _rec_inputs():
        import jax
        import jax.numpy as jnp
        _rk = jax.random.key(seed)
        x = -0.0003929 + 0.9999 * jax.random.normal(jax.random.fold_in(_rk, 1), (8, 128, 512), jnp.float32)
        _lenS = 128 - jax.random.randint(jax.random.fold_in(_rk, 7), (8,), 0, max(1, 128 // 4) + 1, jnp.int32)
        _lenS2 = 128 - jax.random.randint(jax.random.fold_in(_rk, 8), (8,), 0, max(1, 128 // 4) + 1, jnp.int32)
        _ctx_4096P = jax.random.normal(jax.random.fold_in(_rk, 11), (8, 16, 512), jnp.float32)
        _ctx_4096c = jax.random.dirichlet(jax.random.fold_in(_rk, 511), 0.3 * jnp.ones((16,), jnp.float32), (8, 128))
        _ctx_4096t = jnp.einsum('bsk,bkd->bsd', _ctx_4096c, _ctx_4096P)
        _ctx_4096t = _ctx_4096t * jax.lax.rsqrt(jnp.mean(jnp.square(_ctx_4096t)) + 1e-12) * 0.953939
        ctx_4096 = 2.81802e-05 + 1.00001 * (_ctx_4096t + 0.3 * jax.random.normal(jax.random.fold_in(_rk, 611), (8, 128, 512), jnp.float32))
        pos_BxS2 = jnp.broadcast_to(jnp.arange(128, dtype=jnp.int32), (8, 128))
        _validS = jnp.arange(128)[None, :] < _lenS[:, None]
        _validS2 = jnp.arange(128)[None, :] < _lenS2[:, None]
        _causal = jnp.tril(jnp.ones((128, 128), dtype=bool))
        mask_BxSxS2_ik0 = jnp.where(jnp.broadcast_to(_validS2[:, None, :], (8, 128, 128)), 0, 1).astype(jnp.int32)
        return (x, ctx_4096, pos_BxS2, mask_BxSxS2_ik0)
    x, ctx_4096, pos_BxS2, mask_BxSxS2_ik0 = _rec_inputs()

    def _L0_xattn_setup():
        import jax, jax.numpy as jnp
        import numpy as np
        B, S, E = (2, 256, 512)
        H, KVH, D = (32, 8, 128)
        GROUPS = H // KVH
        MAX_POS = 512
        ROPE_THETA = 10000.0

        def _rope_tables(max_pos, dim, theta):
            inv_freq = 1.0 / theta ** (jnp.arange(0, dim, 2, dtype=jnp.float32) / dim)
            t = jnp.arange(max_pos, dtype=jnp.float32)
            freqs = jnp.einsum('i,j->ij', t, inv_freq)
            emb = jnp.concatenate([freqs, freqs], axis=-1)
            return (jnp.cos(emb), jnp.sin(emb))

        def _rotate_half(x):
            x1, x2 = (x[..., :x.shape[-1] // 2], x[..., x.shape[-1] // 2:])
            return jnp.concatenate([-x2, x1], axis=-1)
        key = jax.random.key(seed)
        ks = jax.random.split(key, 8)
        scale_w = 1.0 / np.sqrt(E)
        query = jax.random.normal(ks[0], (B, S, E), dtype=jnp.float32)
        k_in = jax.random.normal(ks[1], (B, S, E), dtype=jnp.float32)
        v_in = jax.random.normal(ks[2], (B, S, E), dtype=jnp.float32)
        position_ids = jnp.broadcast_to(jnp.arange(S, dtype=jnp.int64), (B, S))
        src_mask = jnp.tril(jnp.ones((S, S), dtype=jnp.int32))
        src_mask = jnp.broadcast_to(src_mask, (B, S, S))
        Wq = jax.random.normal(ks[3], (E, H * D), dtype=jnp.float32) * scale_w
        Wk = jax.random.normal(ks[4], (E, KVH * D), dtype=jnp.float32) * scale_w
        Wv = jax.random.normal(ks[5], (E, KVH * D), dtype=jnp.float32) * scale_w
        Wo = jax.random.normal(ks[6], (H * D, E), dtype=jnp.float32) * scale_w
        return {'query': query, 'key': k_in, 'value': v_in, 'position_ids': position_ids, 'src_mask': src_mask, 'Wq': Wq, 'Wk': Wk, 'Wv': Wv, 'Wo': Wo}
    _L0_xattn_all = _L0_xattn_setup()
    _L0_xattn_in = {k: v for k, v in _L0_xattn_all.items() if k in ('Wq', 'Wk', 'Wv', 'Wo')}
    del _L0_xattn_all

    def _L0_ffn_setup():
        import jax, jax.numpy as jnp
        import numpy as np
        DIM = 512
        INTER = 128
        E = 16
        GROUPS = 4
        LIM = 2
        K = 2
        SHARED_INTER = 2 * INTER
        SCALE = 1.0
        key = jax.random.key(seed)
        ks = jax.random.split(key, 16)

        def n(k, shape, s=0.02):
            return jax.random.normal(k, shape, jnp.float32) * s
        return {'x': jax.random.normal(ks[0], (1, 256, DIM), jnp.float32), 'router_w': n(ks[1], (DIM, E)), 'router_b': n(ks[2], (E,)), 'router_bias': n(ks[3], (E,), 1.0), 'ew1': n(ks[4], (E, DIM, INTER)), 'eb1': n(ks[5], (E, INTER)), 'ew2': n(ks[6], (E, DIM, INTER)), 'eb2': n(ks[7], (E, INTER)), 'ew3': n(ks[8], (E, INTER, DIM)), 'eb3': n(ks[9], (E, DIM)), 'sw1': n(ks[10], (DIM, SHARED_INTER)), 'sb1': n(ks[11], (SHARED_INTER,)), 'sw2': n(ks[12], (DIM, SHARED_INTER)), 'sb2': n(ks[13], (SHARED_INTER,)), 'sw3': n(ks[14], (SHARED_INTER, DIM)), 'sb3': n(ks[15], (DIM,))}
    _L0_ffn_all = _L0_ffn_setup()
    _L0_ffn_in = {k: v for k, v in _L0_ffn_all.items() if k in ('router_w', 'router_b', 'router_bias', 'ew1', 'eb1', 'ew2', 'eb2', 'ew3', 'eb3', 'sw1', 'sb1', 'sw2', 'sb2', 'sw3', 'sb3')}
    del _L0_ffn_all
    return {'x': x, 'ctx_4096': ctx_4096, 'pos_BxS2': pos_BxS2, 'mask_BxSxS2_ik0': mask_BxSxS2_ik0, 'L0_xattn_Wq': _L0_xattn_in['Wq'], 'L0_xattn_Wk': _L0_xattn_in['Wk'], 'L0_xattn_Wv': _L0_xattn_in['Wv'], 'L0_xattn_Wo': _L0_xattn_in['Wo'], 'L0_ffn_router_w': _L0_ffn_in['router_w'], 'L0_ffn_router_b': _L0_ffn_in['router_b'], 'L0_ffn_router_bias': _L0_ffn_in['router_bias'], 'L0_ffn_ew1': _L0_ffn_in['ew1'], 'L0_ffn_eb1': _L0_ffn_in['eb1'], 'L0_ffn_ew2': _L0_ffn_in['ew2'], 'L0_ffn_eb2': _L0_ffn_in['eb2'], 'L0_ffn_ew3': _L0_ffn_in['ew3'], 'L0_ffn_eb3': _L0_ffn_in['eb3'], 'L0_ffn_sw1': _L0_ffn_in['sw1'], 'L0_ffn_sb1': _L0_ffn_in['sb1'], 'L0_ffn_sw2': _L0_ffn_in['sw2'], 'L0_ffn_sb2': _L0_ffn_in['sb2'], 'L0_ffn_sw3': _L0_ffn_in['sw3'], 'L0_ffn_sb3': _L0_ffn_in['sb3']}

def reference(x, ctx_4096, pos_BxS2, mask_BxSxS2_ik0, L0_xattn_Wq, L0_xattn_Wk, L0_xattn_Wv, L0_xattn_Wo, L0_ffn_router_w, L0_ffn_router_b, L0_ffn_router_bias, L0_ffn_ew1, L0_ffn_eb1, L0_ffn_ew2, L0_ffn_eb2, L0_ffn_ew3, L0_ffn_eb3, L0_ffn_sw1, L0_ffn_sb1, L0_ffn_sw2, L0_ffn_sb2, L0_ffn_sw3, L0_ffn_sb3):
    import jax
    import jax.numpy as jnp

    def _L0_xattn_ref(query, key, value, position_ids, src_mask, Wq, Wk, Wv, Wo):
        import jax, jax.numpy as jnp
        import numpy as np
        B, S, E = (2, 256, 512)
        H, KVH, D = (32, 8, 128)
        GROUPS = H // KVH
        MAX_POS = 512
        ROPE_THETA = 10000.0

        def _rope_tables(max_pos, dim, theta):
            inv_freq = 1.0 / theta ** (jnp.arange(0, dim, 2, dtype=jnp.float32) / dim)
            t = jnp.arange(max_pos, dtype=jnp.float32)
            freqs = jnp.einsum('i,j->ij', t, inv_freq)
            emb = jnp.concatenate([freqs, freqs], axis=-1)
            return (jnp.cos(emb), jnp.sin(emb))

        def _rotate_half(x):
            x1, x2 = (x[..., :x.shape[-1] // 2], x[..., x.shape[-1] // 2:])
            return jnp.concatenate([-x2, x1], axis=-1)
        nb, q_len, _ = query.shape
        q = (query @ Wq).reshape(nb, q_len, H, D).transpose(0, 2, 1, 3)
        k = (key @ Wk).reshape(nb, q_len, KVH, D).transpose(0, 2, 1, 3)
        v = (value @ Wv).reshape(nb, q_len, KVH, D).transpose(0, 2, 1, 3)
        cos_t, sin_t = _rope_tables(MAX_POS, D, ROPE_THETA)
        cos = cos_t[position_ids][:, None]
        sin = sin_t[position_ids][:, None]
        q = q * cos + _rotate_half(q) * sin
        k = k * cos + _rotate_half(k) * sin
        k = jnp.repeat(k, GROUPS, axis=1)
        v = jnp.repeat(v, GROUPS, axis=1)
        scores = jnp.einsum('bhqd,bhkd->bhqk', q, k) / jnp.sqrt(jnp.float32(D))
        mask = src_mask[:, None]
        scores = jnp.where(mask == 0, jnp.float32(-1000000000.0), scores)
        attn = jax.nn.softmax(scores, axis=-1)
        x = jnp.einsum('bhqk,bhkd->bhqd', attn, v)
        x = x.transpose(0, 2, 1, 3).reshape(nb, q_len, H * D)
        return x @ Wo

    def _L0_ffn_ref(x, router_w, router_b, router_bias, ew1, eb1, ew2, eb2, ew3, eb3, sw1, sb1, sw2, sb2, sw3, sb3):
        import jax, jax.numpy as jnp
        import numpy as np
        DIM = 512
        INTER = 128
        E = 16
        GROUPS = 4
        LIM = 2
        K = 2
        SHARED_INTER = 2 * INTER
        SCALE = 1.0
        shape = x.shape
        xt = x.reshape(-1, DIM)
        T = xt.shape[0]
        logits = xt @ router_w + router_b
        scores = jax.nn.softmax(logits.astype(jnp.float32), axis=-1) + router_bias
        g = scores.reshape(T, GROUPS, E // GROUPS)
        _, gidx = jax.lax.top_k(g.max(axis=-1), LIM)
        keep = jnp.zeros((T, GROUPS), bool).at[jnp.arange(T)[:, None], gidx].set(True)
        masked = jnp.where(keep[:, :, None], g, -jnp.inf).reshape(T, E)
        _, idx = jax.lax.top_k(masked, K)
        vals = (jnp.take_along_axis(scores, idx, axis=1) * SCALE).astype(x.dtype)
        gate = jnp.zeros((T, E), x.dtype).at[jnp.arange(T)[:, None], idx].add(vals)

        def step(y, p):
            w1, b1, w2, b2, w3, b3, ge = p
            h = jax.nn.silu(xt @ w1 + b1) * (xt @ w2 + b2)
            return (y + ge[:, None] * (h @ w3 + b3), None)
        y, _ = jax.lax.scan(step, jnp.zeros_like(xt), (ew1, eb1, ew2, eb2, ew3, eb3, gate.T))
        z = jax.nn.silu(xt @ sw1 + sb1) * (xt @ sw2 + sb2) @ sw3 + sb3
        return (y + z).reshape(shape)
    x = x + _L0_xattn_ref(_layernorm(x, axis=-1), ctx_4096, ctx_4096, pos_BxS2, mask_BxSxS2_ik0, L0_xattn_Wq, L0_xattn_Wk, L0_xattn_Wv, L0_xattn_Wo)
    x = x + _L0_ffn_ref(_layernorm(x, axis=-1), L0_ffn_router_w, L0_ffn_router_b, L0_ffn_router_bias, L0_ffn_ew1, L0_ffn_eb1, L0_ffn_ew2, L0_ffn_eb2, L0_ffn_ew3, L0_ffn_eb3, L0_ffn_sw1, L0_ffn_sb1, L0_ffn_sw2, L0_ffn_sb2, L0_ffn_sw3, L0_ffn_sb3)
    return x

_drawn_inputs = setup_inputs


def setup_inputs(seed=0):
    import zlib

    import numpy as np

    out = dict(_drawn_inputs(seed))
    spreads = {}
    factors = {'L0_ffn_router_w': 23.108,
     'L0_ffn_router_b': 200.0,
     'L0_ffn_eb1': 43.513,
     'L0_ffn_eb2': 44.575,
     'L0_ffn_sw1': 3.435,
     'L0_ffn_sb1': 8.0,
     'L0_ffn_sw2': 3.405,
     'L0_ffn_sb2': 8.0,
     'L0_ffn_sw3': 3.442,
     'L0_ffn_sb3': 5.874}
    for name, (base, spread) in spreads.items():
        noise = np.random.default_rng([zlib.crc32(name.encode()), seed]).standard_normal(out[name].shape)
        drawn = base * np.exp(spread * noise) if base else spread * noise
        out[name] = jnp.asarray(drawn.astype(out[name].dtype))
    for name, factor in factors.items():
        out[name] = (out[name] * factor).astype(out[name].dtype)
    return out
```

```python
from contextlib import ExitStack

import numpy as np

import concourse.bass as bass
from concourse import mybir
from concourse.alu_op_type import AluOpType as ALU

ACT = mybir.ActivationFunctionType
AX_X = mybir.AxisListType.X
F32 = mybir.dt.float32
F32R = mybir.dt.float32r
I32 = mybir.dt.int32

P = 128
B = 8
E = 512
C = E // P
T = B * P
NH = 32
G = 8
J = NH // G
HALF = T // 2
TPH = B // 2
MAX_POS = 512
PC = MAX_POS // P
THETA = 10000.0
NE = 16
NX = 18
RG = 4
EPG = NE // RG
SCALE = 1.0 / float(np.sqrt(np.float32(P)))
MASKED = -1.0e9
HUGE = 3.0e38
EPS = 1e-5
OUT_OF_REACH = 1.0e30

PROJECTIONS = [
    ("Q", 0, 0), ("Q", 0, 1), ("VT", 0, 0), ("V", 0, 0), ("Q", 0, 2), ("Q", 0, 3), ("K", 0, 0),
    ("K", 1, 0), ("Q", 1, 0), ("VT", 1, 0), ("Q", 1, 1), ("V", 1, 0), ("Q", 1, 2), ("Q", 1, 3),
]
NP = len(PROJECTIONS)
STEP_OF = [4, 5, 5, 6, 6, 7, 8, 8, 9, 10, 10, 10, 10, 10]
STEPS = 11
WEIGHTS = ["q0", "q1", "v", "q2", "q3", "k"]
NW = len(WEIGHTS)
ROPED = [k in ("Q", "K") for k, _, _ in PROJECTIONS]


def weight_of(kind, j):
    return WEIGHTS.index({"Q": f"q{j}", "K": "k", "VT": "v"}[kind])


def build(nc, x, ctx_in, pos, mask, wq, wkv, wo, rw, rb, rbias, w12, w3, b3, rope, iota, ident_in, out):
    with ExitStack() as stack:
        def sb(name, shape, dt=F32):
            return stack.enter_context(nc.sbuf_tensor(f"sb_{name}", shape, dt))

        def sem(name):
            return stack.enter_context(nc.semaphore(f"s_{name}"))

        bank = [stack.enter_context(nc.psum_tensor(f"bank{i}_ps", [P, 512], F32)) for i in range(8)]

        acc = sb("acc", [P, B, E])
        act_hi = sb("act_hi", [P, C, T], F32R)
        act_lo = sb("act_lo", [P, C, T], F32R)
        ctx_hi = sb("ctx_hi", [P, C, T], F32R)
        ctx_lo = sb("ctx_lo", [P, C, T], F32R)
        cap = sb("cap", [P, B, P])
        cos_t = sb("cos_t", [P, T])
        sin_t = sb("sin_t", [P, T])
        q_t = sb("q_t", [P, J, T])
        k_t = sb("k_t", [P, T])
        v_t = sb("v_t", [P, HALF])
        v_hi = sb("v_hi", [P, B, P], F32R)
        v_lo = sb("v_lo", [P, B, P], F32R)
        wq_raw = sb("wq_raw", [P, J, C, P])
        wq_hi = sb("wq_hi", [P, J, C, P], F32R)
        wq_lo = sb("wq_lo", [P, J, C, P], F32R)
        wkv_raw = sb("wkv_raw", [P, 2, C, P])
        wkv_hi = sb("wkv_hi", [P, 2, C, P], F32R)
        wkv_lo = sb("wkv_lo", [P, 2, C, P], F32R)
        wo_raw = sb("wo_raw", [P, J, E])
        wo_hi = sb("wo_hi", [P, J, E], F32R)
        wo_lo = sb("wo_lo", [P, J, E], F32R)
        capped = sb("capped", [P, 2, J, P])
        probs = sb("probs", [P, 2, J, P])
        probs_hi = sb("probs_hi", [P, J * P], F32R)
        probs_lo = sb("probs_lo", [P, J * P], F32R)
        o_hi = sb("o_hi", [P, J, P], F32R)
        o_lo = sb("o_lo", [P, J, P], F32R)
        rope_a = sb("rope_a", [P, 2, HALF])
        rope_b = sb("rope_b", [P, 2, HALF])
        neg_max = sb("neg_max", [P, 2, J])
        row_sum = sb("row_sum", [P, 2, J])
        row_inv = sb("row_inv", [P, 2, J])
        ident = sb("ident", [P, P])
        iota_t = sb("iota_t", [P, PC])
        stats = sb("stats", [P, B, 6])
        mean_var = sb("mean_var", [P, B, 2])
        var_eps = sb("var_eps", [P, B])
        std = sb("std", [P, B])
        rstd = sb("rstd", [P, B])
        tmp8 = sb("tmp8", [P, B])
        rw_hi = sb("rw_hi", [P, C, NE], F32R)
        rw_lo = sb("rw_lo", [P, C, NE], F32R)
        normed = q_t[:, :, :].rearrange("p j (a e) -> p (j a) e", e=E)
        ctx_raw = wq_raw[:, :, :, :].rearrange("p j c n -> p j (c n)")
        rope_tab = wo_raw[:, 0:2, :].rearrange("p a (c n) -> p a c n", n=P)
        one_hot = wo_raw[:, 2:4, :]
        pos_f = probs[:, :, :, :].rearrange("p a j n -> p (a j n)")
        pos_i = capped[:, :, :, :].rearrange("p a j n -> p (a j n)").bitcast(I32)
        mask_i = rope_a[:, :, :].rearrange("p a (b k) -> p (a b) k", k=P).bitcast(I32)
        r1, r2, r3, r4 = (probs[:, i // 2, 2 * (i % 2), :].rearrange("p (b e) -> p b e", e=NE) for i in range(4))
        after = wkv_raw[:, :, :, :].rearrange("p a c n -> p (a c n)")
        rw_sb = after[:, 0:C * NE].rearrange("p (c e) -> p c e", c=C)
        rb_sb = after[:, 64:64 + NE]
        rbias_sb = after[:, 96:96 + NE]
        gates = after[:, 256:256 + B * NX].rearrange("p (b e) -> p b e", b=B)
        firsts = after[:, 112:112 + NE]
        s8 = after[:, 400:400 + B]
        cmp8 = after[:, 408:408 + B]
        gmax = after[:, 416:416 + B * RG].rearrange("p (b g) -> p b g", b=B)
        keep = after[:, 448:448 + B * RG].rearrange("p (b g) -> p b g", b=B)
        silu_t = rope_a
        h_t = rope_b
        h_hi = ctx_hi[:, 0:2, 0:HALF]
        h_lo = ctx_lo[:, 0:2, 0:HALF]
        gates_t = k_t[0:NE + 1, :]
        b3_sb = v_t[0:NE + 1, :]
        ew_raw, ew_hi, ew_lo = wq_raw, wq_hi, wq_lo
        ew3_raw, ew3_hi, ew3_lo = wo_raw[:, :, :].rearrange("p j e -> p (j e)"), wo_hi, wo_lo

        x_loaded = [sem(f"x_loaded{h}") for h in range(2)]
        ctx_loaded = [sem(f"ctx_loaded{h}") for h in range(2)]
        pos_loaded = sem("pos_loaded")
        mask_loaded = sem("mask_loaded")
        consts_loaded = sem("consts_loaded")
        rope_loaded = sem("rope_loaded")
        router_loaded = sem("router_loaded")
        wqkv_loaded = sem("wqkv_loaded")
        wo_loaded = sem("wo_loaded")
        chain = sem("chain")
        std_ready = sem("std_ready")
        var_ready = sem("var_ready")
        normed_ready = sem("normed_ready")
        turned = sem("turned")
        turned_hi = sem("turned_hi")
        turned_split = sem("turned_split")
        hot_ready = sem("hot_ready")
        hot_used = sem("hot_used")
        b3_loaded = sem("b3_loaded")
        trig_ready = sem("trig_ready")
        cap_ready = sem("cap_ready")
        wqkv_hi = sem("wqkv_hi")
        wqkv_split = sem("wqkv_split")
        wo_hi_done = sem("wo_hi_done")
        wo_split = sem("wo_split")
        proj_ready = sem("proj_ready")
        proj_written = sem("proj_written")
        proj_hi = sem("proj_hi")
        rope_parts = sem("rope_parts")
        scores_ready = sem("scores_ready")
        scores_capped = sem("scores_capped")
        max_ready = sem("max_ready")
        exp_done = sem("exp_done")
        inv_ready = sem("inv_ready")
        probs_ready = sem("probs_ready")
        probs_turned = sem("probs_turned")
        probs_hi_done = sem("probs_hi_done")
        probs_split = sem("probs_split")
        o_ready = sem("o_ready")
        o_hi_done = sem("o_hi_done")
        o_split = sem("o_split")
        out_ready = sem("out_ready")
        out_added = sem("out_added")
        logits_ready = sem("logits_ready")
        route_max = sem("route_max")
        route_exp = sem("route_exp")
        gates_ready = sem("gates_ready")
        gates_turned = sem("gates_turned")
        gates_copied = sem("gates_copied")
        rw_split = sem("rw_split")
        bias_ready = sem("bias_ready")
        bias_added = sem("bias_added")
        ew_loaded = sem("ew_loaded")
        ew3_loaded = sem("ew3_loaded")
        ew_hi_done = sem("ew_hi_done")
        ew_split = sem("ew_split")
        ew3_hi_done = sem("ew3_hi_done")
        ew3_split = sem("ew3_split")
        h1_ready = sem("h1_ready")
        h2_ready = sem("h2_ready")
        silu_done = sem("silu_done")
        h_done = sem("h_done")
        h_hi_done = sem("h_hi_done")
        h_split = sem("h_split")
        y_ready = sem("y_ready")
        y_added = sem("y_added")
        stored = sem("stored")

        def half(h):
            return slice(h * HALF, (h + 1) * HALF)

        def tile_cols(b):
            return slice(b * P, (b + 1) * P)

        def in_step(s):
            return s < B, 1 <= s <= B, 2 <= s <= B + 1

        block = stack.enter_context(nc.Block())

        @block.sync
        def _(sp):
            for h in range(2):
                sp.dma_start(acc[:, h * TPH:(h + 1) * TPH, :], x[:, h * TPH:(h + 1) * TPH, :]).then_inc(x_loaded[h], 16)
            sp.dma_start(ident[:], ident_in).then_inc(consts_loaded, 16)
            sp.dma_start(iota_t[:], iota).then_inc(consts_loaded, 16)
            sp.dma_start(pos_i, pos).then_inc(pos_loaded, 16)
            sp.dma_start(rope_tab, rope).then_inc(rope_loaded, 16)
            sp.dma_start(ctx_raw, ctx_in[:, 0:TPH, :]).then_inc(ctx_loaded[0], 16)
            sp.dma_start(mask_i, mask).then_inc(mask_loaded, 16)
            sp.dma_start(wkv_raw[:], wkv[0]).then_inc(wqkv_loaded, 16)
            sp.wait_ge(turned, TPH)
            sp.dma_start(ctx_raw, ctx_in[:, TPH:B, :]).then_inc(ctx_loaded[1], 16)
            sp.wait_ge(turned, B)
            sp.dma_start(wq_raw[:], wq[0]).then_inc(wqkv_loaded, 16)
            sp.wait_ge(hot_used, 2 * PC)
            sp.dma_start(wo_raw[:], wo[0]).then_inc(wo_loaded, 16)
            with sp.Fori(1, G) as g:
                sp.wait_ge(wqkv_split, g * NW)
                sp.dma_start(wq_raw[:], wq[bass.ds(g, 1)].rearrange("a p j c n -> p (a j) c n")).then_inc(wqkv_loaded, 16)
                sp.dma_start(wkv_raw[:], wkv[bass.ds(g, 1)].rearrange("a p j c n -> p (a j) c n")).then_inc(wqkv_loaded, 16)
                sp.wait_ge(wo_split, g * J)
                sp.dma_start(wo_raw[:], wo[bass.ds(g, 1)].rearrange("a p j n -> p (a j) n")).then_inc(wo_loaded, 16)
            sp.wait_ge(wqkv_split, G * NW)
            sp.dma_start(rw_sb, rw).then_inc(router_loaded, 16)
            sp.dma_start(rb_sb, rb).then_inc(router_loaded, 16)
            sp.dma_start(rbias_sb, rbias).then_inc(router_loaded, 16)
            sp.dma_start(ew_raw[:, 0:2], w12[0]).then_inc(ew_loaded, 16)
            sp.wait_ge(wo_split, G * J)
            sp.dma_start(ew3_raw[:, 0:E + 2], w3[0]).then_inc(ew3_loaded, 16)
            sp.wait_ge(proj_ready, G * NP)
            sp.dma_start(b3_sb, b3).then_inc(b3_loaded, 16)
            with sp.Fori(1, NX) as e:
                sp.wait_ge(ew_split, e * 2)
                sp.dma_start(ew_raw[:, 0:2], w12[bass.ds(e, 1)].rearrange("a p j c n -> p (a j) c n")).then_inc(ew_loaded, 16)
                sp.wait_ge(ew3_split, e)
                sp.wait_ge(h_done, e * 2)
                sp.dma_start(ew3_raw[:, 0:E + 2], w3[bass.ds(e, 1)].rearrange("a p n -> p (a n)")).then_inc(ew3_loaded, 16)
            for b in range(B):
                sp.wait_ge(y_added, (NX - 1) * B + b + 1)
                sp.dma_start(out[:, b, :], acc[:, b, :]).then_inc(stored, 16)
            sp.wait_ge(stored, B * 16)

        @block.tensor
        def _(pe):
            def product(out_ap, st_hi, st_lo, mv_hi, mv_lo, first, last):
                pe.matmul(out_ap, st_lo, mv_hi, start=first, stop=False)
                pe.matmul(out_ap, st_hi, mv_lo, start=False, stop=False)
                return pe.matmul(out_ap, st_hi, mv_hi, start=False, stop=last)

            def project(n, g):
                kind, h, j = PROJECTIONS[n]
                if not (isinstance(g, int) and g == 0 and n < 2):
                    pe.wait_ge(proj_written, g * NP + (n - 1))
                dst = bank[n % 2]
                if kind == "V":
                    for i in range(TPH):
                        if i == 0:
                            pe.wait_ge(proj_written, g * NP + PROJECTIONS.index(("VT", h, 0)) + 1)
                        ins = pe.transpose(dst[:, tile_cols(i)], v_t[:, tile_cols(i)], ident[:, :])
                    ins.then_inc(proj_ready, 1)
                    return
                w = weight_of(kind, j)
                if h == 0 or (kind, h) == ("K", 1):
                    pe.wait_ge(wqkv_split, g * NW + w + 1)
                w_hi, w_lo = (wq_hi, wq_lo) if kind == "Q" else (wkv_hi, wkv_lo)
                slot = {"Q": j, "K": 0, "VT": 1}[kind]
                m_hi, m_lo = (act_hi, act_lo) if kind == "Q" else (ctx_hi, ctx_lo)
                for c in range(C):
                    ins = product(dst[:, :], w_hi[:, slot, c, :], w_lo[:, slot, c, :],
                                  m_hi[:, c, half(h)], m_lo[:, c, half(h)], c == 0, c == C - 1)
                ins.then_inc(proj_ready, 1)

            def turn_tile(src, n, ready, at):
                pe.wait_ge(ready, at)
                if n >= 2:
                    pe.wait_ge(turned_split, n - 1)
                for c in range(C):
                    ins = pe.transpose(bank[n % 2][:, tile_cols(c)], src[:, c * P:(c + 1) * P], ident[:, :])
                ins.then_inc(turned, 1)

            def attend(g, last):
                for s in range(STEPS):
                    a, t, w = in_step(s)
                    if a:
                        if s in (0, TPH):
                            need = max(n for n, (k, h, _) in enumerate(PROJECTIONS) if h == s // TPH and k != "VT")
                            pe.wait_ge(proj_written, g * NP + need + 1)
                        if not (isinstance(g, int) and g == 0 and s < 2):
                            pe.wait_ge(scores_capped, g * B + s - 1)
                        for j in range(J):
                            ins = pe.matmul(bank[2 + s % 2][:, tile_cols(j)], q_t[:, j, tile_cols(s)],
                                            k_t[:, tile_cols(s)], start=True, stop=True)
                        ins.then_inc(scores_ready, 1)
                    if t:
                        b = s - 1
                        pe.wait_ge(probs_ready, g * B + b + 1)
                        for j in range(J):
                            ins = pe.transpose(bank[4][:, tile_cols(j)], probs[:, b % 2, j, :], ident[:, :])
                        ins.then_inc(probs_turned, 1)
                    if w:
                        b = s - 2
                        pe.wait_ge(o_split, g * B + b + 1)
                        if b == 0:
                            pe.wait_ge(wo_split, g * J + J)
                        if not (isinstance(g, int) and g == 0 and b < 2):
                            pe.wait_ge(out_added, g * B + b - 1)
                        for j in range(J):
                            ins = product(bank[6 + b % 2][:, :], o_hi[:, j, :], o_lo[:, j, :],
                                          wo_hi[:, j, :], wo_lo[:, j, :], j == 0, j == J - 1)
                        ins.then_inc(out_ready, 1)
                    if t:
                        b = s - 1
                        pe.wait_ge(probs_split, g * B + b + 1)
                        product(bank[5][:, :], v_hi[:, b, :], v_lo[:, b, :], probs_hi[:, :], probs_lo[:, :],
                                True, True).then_inc(o_ready, 1)
                    if not last:
                        for n in range(NP):
                            if STEP_OF[n] == s:
                                project(n, g + 1)

            pe.wait_ge(consts_loaded, 32)
            for b in range(B):
                turn_tile(ctx_raw[:, b % TPH, :], b, ctx_loaded[b // TPH], 16)
            pe.wait_ge(rope_loaded, 16)
            for h in range(2):
                for c in range(PC):
                    pe.wait_ge(hot_ready, h * PC + c + 1)
                    for a in range(2):
                        ins = pe.matmul(bank[2 + 2 * h + a][:, :], rope_tab[:, a, c, :], one_hot[:, c % 2, :],
                                        start=(c == 0), stop=(c == PC - 1))
                    ins.then_inc(hot_used, 1)
            for b in range(B):
                turn_tile(normed[:, b, :], B + b, normed_ready, b + 1)
            pe.wait_ge(turned_split, 2 * B)
            pe.wait_ge(trig_ready, 4)
            for n in range(NP):
                project(n, 0)
            attend(0, False)
            with pe.Fori(1, G - 1) as g:
                attend(g, False)
            attend(G - 1, True)

            for b in range(B):
                turn_tile(normed[:, b, :], 2 * B + b, normed_ready, B + b + 1)
            pe.wait_ge(turned_split, 3 * B)
            pe.wait_ge(rw_split, 1)
            for b in range(B):
                k = 0
                for c in range(C):
                    for st in (act_lo, act_hi):
                        for mv in (rw_lo, rw_hi):
                            ins = pe.matmul(bank[2][:, b * NE:(b + 1) * NE], st[:, c, tile_cols(b)], mv[:, c, :],
                                            start=(k == 0), stop=(k == 4 * C - 1))
                            k += 1
            ins.then_inc(logits_ready, 1)

            def expert_h(e, h):
                if h == 0:
                    pe.wait_ge(ew_split, e * 2 + 2)
                if not (isinstance(e, int) and e == 0):
                    pe.wait_ge(h_done, e * 2 + h - 1)
                for a, ready in ((0, h1_ready), (1, h2_ready)):
                    for c in range(C):
                        ins = product(bank[2 * h + a][:, :], ew_hi[:, a, c, :], ew_lo[:, a, c, :],
                                      act_hi[:, c, half(h)], act_lo[:, c, half(h)], c == 0, c == C - 1)
                    ins.then_inc(ready, 1)

            def expert_y(e, b):
                if b == 0:
                    pe.wait_ge(ew3_split, e + 1)
                if b % TPH == 0:
                    pe.wait_ge(h_split, e * 2 + b // TPH + 1)
                if not (isinstance(e, int) and e == 0 and b < 4):
                    pe.wait_ge(y_added, e * B + b - 3)
                product(bank[4 + b % 4][:, :], h_hi[:, b // TPH, tile_cols(b % TPH)], h_lo[:, b // TPH, tile_cols(b % TPH)],
                        ew3_hi[:, 0, :], ew3_lo[:, 0, :], True, True).then_inc(y_ready, 1)

            def expert(e, also=None):
                expert_h(e, 0)
                if also:
                    also()
                expert_h(e, 1)
                for b in range(B):
                    expert_y(e, b)

            def output_biases():
                pe.wait_ge(gates_ready, 1)
                for b in range(B):
                    ins = pe.transpose(bank[4 + b // TPH][0:NE + 1, tile_cols(b % TPH)], gates[:, b, 0:NE + 1], ident[:, :])
                ins.then_inc(gates_turned, 1)
                pe.wait_ge(gates_copied, 1)
                pe.wait_ge(b3_loaded, 16)
                for b in range(B):
                    if b >= 2:
                        pe.wait_ge(bias_added, b - 1)
                    pe.matmul(bank[6 + b % 2][:, :], gates_t[:, tile_cols(b)], b3_sb, start=True, stop=True).then_inc(bias_ready, 1)
                pe.wait_ge(bias_added, B)

            expert(0, output_biases)
            with pe.Fori(1, NX) as e:
                expert(e)

        @block.scalar
        def _(act):
            def std_of(n):
                cols = slice((n - 1) % 2 * TPH, ((n - 1) % 2 + 1) * TPH)
                act.wait_ge(var_ready, n)
                nc.scalar.activation(std[:, cols], var_eps[:, cols], ACT.Sqrt).then_inc(std_ready, 1)

            def turn_hi(n, dst):
                act.wait_ge(turned, n + 1)
                nc.scalar.copy(dst, bank[n % 2][:, :].rearrange("p (c t) -> p c t", c=C)).then_inc(turned_hi, 1)

            def split_qkv(i, g):
                w = WEIGHTS[i]
                if w[0] == "q":
                    src, dst = wq_raw[:, int(w[1])], wq_hi[:, int(w[1])]
                else:
                    src, dst = wkv_raw[:, "kv".index(w)], wkv_hi[:, "kv".index(w)]
                if i == 0:
                    act.wait_ge(wqkv_loaded, g * 32 + 32)
                    if not (isinstance(g, int) and g == 0):
                        act.wait_ge(proj_ready, g * NP)
                nc.scalar.copy(dst, src).then_inc(wqkv_hi, 1)

            def split_wo(j, g):
                if j == 0:
                    act.wait_ge(wo_loaded, g * 16 + 16)
                    if not (isinstance(g, int) and g == 0):
                        act.wait_ge(out_ready, g * B)
                nc.scalar.copy(wo_hi[:, j, :], wo_raw[:, j, :]).then_inc(wo_hi_done, 1)

            def project_hi(n, g):
                kind, h, j = PROJECTIONS[n]
                if kind == "V":
                    act.wait_ge(proj_ready, g * NP + n + 1)
                    nc.scalar.copy(v_hi[:, h * TPH:(h + 1) * TPH, :],
                                   bank[n % 2][:, :].rearrange("p (b d) -> p b d", d=P)).then_inc(proj_hi, 1)

            def attend(g, last):
                for s in range(STEPS):
                    a, t, w = in_step(s)
                    if t:
                        act.wait_ge(probs_turned, g * B + s)
                        nc.scalar.copy(probs_hi[:, :], bank[4][:, :]).then_inc(probs_hi_done, 1)
                    if a:
                        act.wait_ge(max_ready, g * B + s + 1)
                        for j in range(J):
                            ins = nc.scalar.activation(probs[:, s % 2, j, :], capped[:, s % 2, j, :], ACT.Exp,
                                                       bias=neg_max[:, s % 2, j:j + 1], scale=1.0,
                                                       accum_out=row_sum[:, s % 2, j:j + 1])
                        ins.then_inc(exp_done, 1)
                    if t:
                        act.wait_ge(o_ready, g * B + s)
                        nc.scalar.copy(o_hi[:, :, :], bank[5][:, :].rearrange("p (j t) -> p j t", j=J)).then_inc(o_hi_done, 1)
                    if not last:
                        if s < 3:
                            for i in (2 * s, 2 * s + 1):
                                split_qkv(i, g + 1)
                        if s == B + 1:
                            for j in range(J):
                                split_wo(j, g + 1)
                        for n in range(NP):
                            if STEP_OF[n] == s:
                                project_hi(n, g + 1)

            for h in range(2):
                std_of(h + 1)
            for b in range(B):
                turn_hi(b, ctx_hi[:, :, tile_cols(b)])
            for b in range(B):
                turn_hi(B + b, act_hi[:, :, tile_cols(b)])
            for i in range(NW):
                split_qkv(i, 0)
            for j in range(J):
                split_wo(j, 0)
            for n in range(NP):
                project_hi(n, 0)
            attend(0, False)
            with act.Fori(1, G - 1) as g:
                attend(g, False)
            attend(G - 1, True)

            def expert_w(e):
                act.wait_ge(ew_loaded, e * 16 + 16)
                act.wait_ge(h2_ready, e * 2)
                for a in range(2):
                    nc.scalar.copy(ew_hi[:, a], ew_raw[:, a]).then_inc(ew_hi_done, 1)

            def expert_w3(e):
                act.wait_ge(ew3_loaded, e * 16 + 16)
                if not (isinstance(e, int) and e == 0):
                    act.wait_ge(y_ready, e * B)
                nc.scalar.copy(ew3_hi[:, 0, :], ew3_raw[:, 0:E]).then_inc(ew3_hi_done, 1)

            def expert(e):
                expert_w3(e)
                for h in range(2):
                    act.wait_ge(h1_ready, e * 2 + h + 1)
                    nc.scalar.activation(silu_t[:, h, :], bank[2 * h][:, :], ACT.Silu,
                                         bias=ew3_raw[:, E:E + 1], scale=1.0).then_inc(silu_done, 1)
                    act.wait_ge(h_done, e * 2 + h + 1)
                    nc.scalar.copy(h_hi[:, h, :], h_t[:, h, :]).then_inc(h_hi_done, 1)

            for h in range(2):
                std_of(2 + h + 1)
            for b in range(B):
                turn_hi(2 * B + b, act_hi[:, :, tile_cols(b)])
            act.wait_ge(router_loaded, 48)
            act.wait_ge(ew_loaded, 16)
            for a in range(2):
                nc.scalar.copy(ew_hi[:, a], ew_raw[:, a]).then_inc(ew_hi_done, 1)
            act.wait_ge(route_max, 1)
            nc.scalar.activation(r2, r1, ACT.Exp).then_inc(route_exp, 1)
            expert(0)
            expert_w(1)
            with act.Fori(1, NX - 1) as e:
                expert(e)
                expert_w(e + 1)
            expert(NX - 1)

        @block.gpsimd
        def _(pool):
            def low(dst, raw, hi):
                return nc.gpsimd.tensor_tensor(dst, raw, hi.bitcast(F32), ALU.subtract)

            def split_qkv(g):
                for i, w in enumerate(WEIGHTS):
                    pool.wait_ge(wqkv_hi, g * NW + i + 1)
                    if w[0] == "q":
                        j = int(w[1])
                        ins = low(wq_lo[:, j], wq_raw[:, j], wq_hi[:, j])
                    else:
                        a = "kv".index(w)
                        ins = low(wkv_lo[:, a], wkv_raw[:, a], wkv_hi[:, a])
                    ins.then_inc(wqkv_split, 1)

            def split_wo(g):
                for j in range(J):
                    pool.wait_ge(wo_hi_done, g * J + j + 1)
                    low(wo_lo[:, j, :], wo_raw[:, j, :], wo_hi[:, j, :]).then_inc(wo_split, 1)

            split_qkv(0)
            split_wo(0)
            with pool.Fori(1, G) as g:
                split_qkv(g)
                split_wo(g)
            with pool.Fori(0, NX) as e:
                for a in range(2):
                    pool.wait_ge(ew_hi_done, e * 2 + a + 1)
                    low(ew_lo[:, a], ew_raw[:, a], ew_hi[:, a]).then_inc(ew_split, 1)
                pool.wait_ge(ew3_hi_done, e + 1)
                low(ew3_lo[:, 0, :], ew3_raw[:, 0:E], ew3_hi[:, 0, :]).then_inc(ew3_split, 1)

        @block.vector
        def _(dve):
            count = [0]

            def link(ins):
                count[0] += 1
                ins.then_inc(chain, 1)
                dve.wait_ge(chain, count[0])

            def layernorm(first, loaded):
                for h in range(2):
                    if loaded:
                        dve.wait_ge(loaded[h], 16)
                    tiles = range(h * TPH, (h + 1) * TPH)
                    cols = slice(h * TPH, (h + 1) * TPH)
                    for b in tiles:
                        last = nc.vector.bn_stats(stats[:, b, :], acc[:, b, :])
                    link(last)
                    for b in tiles:
                        last = nc.vector.bn_aggr(mean_var[:, b, :], stats[:, b, :])
                    link(last)
                    nc.vector.tensor_scalar(var_eps[:, cols], mean_var[:, cols, 1], EPS, None, ALU.add).then_inc(var_ready, 1)
                    dve.wait_ge(std_ready, first // TPH + h + 1)
                    link(nc.vector.reciprocal(rstd[:, cols], std[:, cols]))
                    link(nc.vector.tensor_tensor(tmp8[:, cols], rstd[:, cols], rstd[:, cols], ALU.mult))
                    link(nc.vector.tensor_tensor(tmp8[:, cols], tmp8[:, cols], var_eps[:, cols], ALU.mult))
                    link(nc.vector.tensor_scalar(tmp8[:, cols], tmp8[:, cols], -0.5, 1.5, ALU.mult, ALU.add))
                    link(nc.vector.tensor_tensor(rstd[:, cols], tmp8[:, cols], rstd[:, cols], ALU.mult))
                    for b in tiles:
                        nc.vector.tensor_scalar(normed[:, b, :], acc[:, b, :], mean_var[:, b, 0:1], rstd[:, b:b + 1],
                                                ALU.subtract, ALU.mult).then_inc(normed_ready, 1)

            def turn_lo(n, hi, lo):
                dve.wait_ge(turned_hi, n + 1)
                nc.vector.tensor_tensor(lo, bank[n % 2][:, :].rearrange("p (c t) -> p c t", c=C), hi.bitcast(F32),
                                        ALU.subtract).then_inc(turned_split, 1)

            def project_out(n, g, roped):
                kind, h, j = PROJECTIONS[n]
                dve.wait_ge(proj_ready, g * NP + n + 1)
                src = bank[n % 2]
                if kind == "VT":
                    nc.vector.tensor_copy(v_t[:, :], src[:, :]).then_inc(proj_written, 1)
                elif kind == "V":
                    dve.wait_ge(proj_hi, g * 2 + h + 1)
                    tiles = slice(h * TPH, (h + 1) * TPH)
                    nc.vector.tensor_tensor(v_lo[:, tiles, :], src[:, :].rearrange("p (b d) -> p b d", d=P),
                                            v_hi[:, tiles, :].bitcast(F32), ALU.subtract).then_inc(proj_written, 1)
                else:
                    r = roped % 2
                    D2 = P // 2
                    nc.vector.tensor_tensor(rope_a[:, r, :], src[:, :], cos_t[:, half(h)], ALU.mult)
                    nc.vector.tensor_tensor(rope_b[D2:P, r, :], src[0:D2, :], sin_t[0:D2, half(h)], ALU.mult)
                    nc.vector.tensor_tensor(rope_b[0:D2, r, :], src[D2:P, :], sin_t[D2:P, half(h)],
                                            ALU.mult).then_inc(rope_parts, 1)
                    dve.wait_ge(rope_parts, g * sum(ROPED) + roped + 1)
                    dst = q_t[:, j, half(h)] if kind == "Q" else k_t[:, half(h)]
                    nc.vector.tensor_tensor(dst, rope_a[:, r, :], rope_b[:, r, :], ALU.add).then_inc(proj_written, 1)

            def attend(g, last):
                for s in range(STEPS):
                    a, t, w = in_step(s)
                    if a:
                        dve.wait_ge(scores_ready, g * B + s + 1)
                        nc.vector.scalar_tensor_tensor(
                            out=capped[:, s % 2, :, :], in0=bank[2 + s % 2][:, :].rearrange("p (j k) -> p j k", j=J),
                            scalar=SCALE, in1=cap[:, s:s + 1, :].to_broadcast([P, J, P]), op0=ALU.mult,
                            op1=ALU.min).then_inc(scores_capped, 1)
                        dve.wait_ge(scores_capped, g * B + s + 1)
                        nc.vector.tensor_reduce(neg_max[:, s % 2, :], capped[:, s % 2, :, :], AX_X, ALU.max,
                                                negate=True).then_inc(max_ready, 1)
                    if t:
                        dve.wait_ge(probs_hi_done, g * B + s)
                        nc.vector.tensor_tensor(probs_lo[:, :], bank[4][:, :], probs_hi[:, :].bitcast(F32),
                                                ALU.subtract).then_inc(probs_split, 1)
                    if w:
                        b = s - 2
                        dve.wait_ge(out_ready, g * B + b + 1)
                        nc.vector.tensor_tensor(acc[:, b, :], acc[:, b, :], bank[6 + b % 2][:, :],
                                                ALU.add).then_inc(out_added, 1)
                    if a:
                        dve.wait_ge(exp_done, g * B + s + 1)
                        nc.vector.reciprocal(row_inv[:, s % 2, :], row_sum[:, s % 2, :]).then_inc(inv_ready, 1)
                        dve.wait_ge(inv_ready, g * B + s + 1)
                        nc.vector.tensor_tensor(probs[:, s % 2, :, :], probs[:, s % 2, :, :],
                                                row_inv[:, s % 2, :].unsqueeze(2).to_broadcast([P, J, P]),
                                                ALU.mult).then_inc(probs_ready, 1)
                    if t:
                        dve.wait_ge(o_hi_done, g * B + s)
                        nc.vector.tensor_tensor(o_lo[:, :, :], bank[5][:, :].rearrange("p (j t) -> p j t", j=J),
                                                o_hi[:, :, :].bitcast(F32), ALU.subtract).then_inc(o_split, 1)
                    if not last:
                        for n in range(NP):
                            if STEP_OF[n] == s:
                                project_out(n, g + 1, sum(ROPED[:n]))

            dve.wait_ge(pos_loaded, 16)
            dve.wait_ge(consts_loaded, 32)
            link(nc.vector.tensor_copy(pos_f, pos_i))
            layernorm(0, x_loaded)
            for b in range(B):
                turn_lo(b, ctx_hi[:, :, tile_cols(b)], ctx_lo[:, :, tile_cols(b)])
            for h in range(2):
                for c in range(PC):
                    n = h * PC + c
                    if n >= 2:
                        dve.wait_ge(hot_used, n - 1)
                    nc.vector.tensor_scalar(one_hot[:, c % 2, :], pos_f[:, half(h)], iota_t[:, c:c + 1], None,
                                            ALU.is_equal).then_inc(hot_ready, 1)
            for h in range(2):
                dve.wait_ge(hot_used, (h + 1) * PC)
                nc.vector.tensor_copy(cos_t[:, half(h)], bank[2 + 2 * h][:, :]).then_inc(trig_ready, 1)
                nc.vector.tensor_copy(sin_t[:, half(h)], bank[3 + 2 * h][:, :]).then_inc(trig_ready, 1)
            dve.wait_ge(mask_loaded, 16)
            link(nc.vector.tensor_scalar(cap[:, :, :], mask_i, 0.0, HUGE, ALU.not_equal, ALU.mult))
            link(nc.vector.tensor_scalar(cap[:, :, :], cap[:, :, :], MASKED, None, ALU.add))
            for b in range(B):
                turn_lo(B + b, act_hi[:, :, tile_cols(b)], act_lo[:, :, tile_cols(b)])
            for n in range(NP):
                project_out(n, 0, sum(ROPED[:n]))
            attend(0, False)
            with dve.Fori(1, G - 1) as g:
                attend(g, False)
            attend(G - 1, True)

            dve.wait_ge(out_added, G * B)
            layernorm(B, None)
            dve.wait_ge(router_loaded, 48)
            link(nc.vector.tensor_copy(rw_hi[:, :, :], rw_sb[:, :, :]))
            nc.vector.tensor_tensor(rw_lo[:, :, :], rw_sb[:, :, :], rw_hi[:, :, :].bitcast(F32),
                                    ALU.subtract).then_inc(rw_split, 1)
            for b in range(B):
                turn_lo(2 * B + b, act_hi[:, :, tile_cols(b)], act_lo[:, :, tile_cols(b)])

            def over(ap, n):
                return ap.unsqueeze(2).to_broadcast([P, B, n])

            dve.wait_ge(logits_ready, 1)
            logits = bank[2][:, 0:B * NE].rearrange("p (b e) -> p b e", e=NE)
            bias_b = rb_sb.unsqueeze(1).to_broadcast([P, B, NE])
            link(nc.vector.tensor_tensor(r3, logits, bias_b, ALU.add))
            link(nc.vector.tensor_reduce(s8, r3, AX_X, ALU.max))
            nc.vector.tensor_tensor(r1, r3, over(s8[:, :], NE), ALU.subtract).then_inc(route_max, 1)
            dve.wait_ge(route_exp, 1)
            link(nc.vector.reduce_sum(s8, r2, AX_X))
            link(nc.vector.reciprocal(tmp8[:], s8))
            link(nc.vector.tensor_tensor(r1, r2, over(tmp8[:, :], NE), ALU.mult))
            link(nc.vector.tensor_tensor(r1, r1, rbias_sb.unsqueeze(1).to_broadcast([P, B, NE]), ALU.add))
            link(nc.vector.tensor_reduce(gmax, r1.rearrange("p b (g e) -> p b g e", e=EPG), AX_X, ALU.max))
            for i in range(RG):
                link(nc.vector.memset(keep[:, :, i], 0.0))
                for k in range(RG):
                    if k != i:
                        link(nc.vector.tensor_tensor(cmp8[:, :], gmax[:, :, k], gmax[:, :, i],
                                                     ALU.is_ge if k < i else ALU.is_gt))
                        link(nc.vector.tensor_tensor(keep[:, :, i], keep[:, :, i], cmp8[:, :], ALU.add))
            link(nc.vector.tensor_scalar(keep, keep, 1.5, None, ALU.is_lt))
            keep_e = keep[:, :, :].unsqueeze(3).to_broadcast([P, B, RG, EPG])

            def v4_of(r):
                return r.rearrange("p b (g e) -> p b g e", e=EPG)

            link(nc.vector.tensor_tensor(v4_of(r3), v4_of(r1), keep_e, ALU.mult))
            link(nc.vector.tensor_scalar(keep, keep, 1.0, OUT_OF_REACH, ALU.subtract, ALU.mult))
            link(nc.vector.tensor_tensor(v4_of(r3), v4_of(r3), keep_e, ALU.add))
            for e in range(NE):
                last = nc.vector.memset(firsts[:, e:e + 1], float(NE - e))
            link(last)
            link(nc.vector.memset(gates[:, :, :], 1.0))
            for k in range(2):
                link(nc.vector.tensor_reduce(s8, r3, AX_X, ALU.max))
                link(nc.vector.tensor_tensor(r2, r3, over(s8[:, :], NE), ALU.is_equal))
                link(nc.vector.tensor_tensor(r2, r2, firsts[:, :].unsqueeze(1).to_broadcast([P, B, NE]), ALU.mult))
                link(nc.vector.tensor_reduce(s8, r2, AX_X, ALU.max))
                link(nc.vector.tensor_tensor(r2, r2, over(s8[:, :], NE), ALU.is_equal))
                if k == 0:
                    link(nc.vector.tensor_copy(r4, r2))
                    link(nc.vector.scalar_tensor_tensor(out=r3, in0=r2, scalar=-HUGE, in1=r3, op0=ALU.mult, op1=ALU.add))
                else:
                    link(nc.vector.tensor_tensor(r4, r4, r2, ALU.add))
            nc.vector.tensor_tensor(gates[:, :, 0:NE], r1, r4, ALU.mult).then_inc(gates_ready, 1)

            def expert(e, also=None):
                for h in range(2):
                    dve.wait_ge(h2_ready, e * 2 + h + 1)
                    dve.wait_ge(silu_done, e * 2 + h + 1)
                    nc.vector.scalar_tensor_tensor(out=h_t[:, h, :], in0=bank[2 * h + 1][:, :],
                                                   scalar=ew3_raw[:, E + 1:E + 2], in1=silu_t[:, h, :],
                                                   op0=ALU.add, op1=ALU.mult).then_inc(h_done, 1)
                    dve.wait_ge(h_hi_done, e * 2 + h + 1)
                    nc.vector.tensor_tensor(h_lo[:, h, :], h_t[:, h, :], h_hi[:, h, :].bitcast(F32),
                                            ALU.subtract).then_inc(h_split, 1)
                for b in range(B):
                    dve.wait_ge(y_ready, e * B + b + 1)
                    nc.vector.scalar_tensor_tensor(out=acc[:, b, :], in0=bank[4 + b % 4][:, :],
                                                   scalar=gates[:, b, bass.ds(e, 1)], in1=acc[:, b, :],
                                                   op0=ALU.mult, op1=ALU.add).then_inc(y_added, 1)

            dve.wait_ge(gates_turned, 1)
            for h in range(2):
                last = nc.vector.tensor_copy(gates_t[:, half(h)], bank[4 + h][0:NE + 1, :])
            last.then_inc(gates_copied, 1)
            for b in range(B):
                dve.wait_ge(bias_ready, b + 1)
                nc.vector.tensor_tensor(acc[:, b, :], acc[:, b, :], bank[6 + b % 2][:, :], ALU.add).then_inc(bias_added, 1)
            dve.wait_ge(bias_added, B)
            with dve.Fori(0, NX) as e:
                expert(e)


def _rope_table():
    inv = (np.float32(1.0) / np.power(np.float32(THETA), np.arange(0, P, 2, dtype=np.float32) / np.float32(P))).astype(np.float32)
    f = np.arange(MAX_POS, dtype=np.float32)[:, None] * inv[None, :]
    cos, sin = np.cos(f).astype(np.float32), np.sin(f).astype(np.float32)
    tab = np.stack([np.concatenate([cos, cos], 1), np.concatenate([sin, -sin], 1)])
    return np.ascontiguousarray(tab.reshape(2, PC, P, P).transpose(2, 0, 1, 3))


def kernel(x, ctx_4096, pos_BxS2, mask_BxSxS2_ik0, L0_xattn_Wq, L0_xattn_Wk, L0_xattn_Wv, L0_xattn_Wo,
           L0_ffn_router_w, L0_ffn_router_b, L0_ffn_router_bias, L0_ffn_ew1, L0_ffn_eb1, L0_ffn_ew2, L0_ffn_eb2,
           L0_ffn_ew3, L0_ffn_eb3, L0_ffn_sw1, L0_ffn_sb1, L0_ffn_sw2, L0_ffn_sb2, L0_ffn_sw3, L0_ffn_sb3):
    import concourse.bacc as bacc
    from concourse.bass_utils import run_bass_kernel_spmd

    a = np.asarray

    def by_expert(routed, shared):
        both = np.concatenate([a(routed), a(shared).reshape(E, 2, P).transpose(1, 0, 2)])
        return both.reshape(NX, C, P, P).transpose(0, 2, 1, 3)

    wk, wv = (a(w).reshape(C, P, G, P).transpose(2, 1, 0, 3) for w in (L0_xattn_Wk, L0_xattn_Wv))
    arrays = {
        "x": a(x).transpose(1, 0, 2),
        "ctx_in": a(ctx_4096).transpose(1, 0, 2),
        "pos": np.broadcast_to(a(pos_BxS2).reshape(1, T), (P, T)),
        "mask": a(mask_BxSxS2_ik0).transpose(1, 0, 2),
        "wq": a(L0_xattn_Wq).reshape(C, P, G, J, P).transpose(2, 1, 3, 0, 4),
        "wkv": np.stack([wk, wv], 2),
        "wo": a(L0_xattn_Wo).reshape(G, J, P, E).transpose(0, 2, 1, 3),
        "rw": a(L0_ffn_router_w).reshape(C, P, NE).transpose(1, 0, 2),
        "rb": np.broadcast_to(a(L0_ffn_router_b), (P, NE)),
        "rbias": np.broadcast_to(a(L0_ffn_router_bias), (P, NE)),
        "w12": np.stack([by_expert(L0_ffn_ew1, L0_ffn_sw1), by_expert(L0_ffn_ew2, L0_ffn_sw2)], 2),
        "w3": np.concatenate([
            np.concatenate([a(L0_ffn_ew3), a(L0_ffn_eb1)[:, :, None], a(L0_ffn_eb2)[:, :, None]], 2),
            np.concatenate([a(L0_ffn_sw3).reshape(2, P, E), a(L0_ffn_sb1).reshape(2, P, 1), a(L0_ffn_sb2).reshape(2, P, 1)], 2),
        ]),
        "b3": np.concatenate([a(L0_ffn_eb3), a(L0_ffn_sb3).reshape(1, E)]),
        "rope": _rope_table(),
        "iota": (np.arange(P)[:, None] + P * np.arange(PC)[None, :]).astype(np.float32),
        "ident": np.eye(P, dtype=np.float32),
    }
    nc = bacc.Bacc("TRN2", target_bir_lowering=False, num_devices=1)
    args = []
    for name, value in arrays.items():
        arrays[name] = value = np.ascontiguousarray(value)
        args.append(nc.dram_tensor(name, value.shape, mybir.dt.from_np(value.dtype), kind="ExternalInput").ap())
    args.append(nc.dram_tensor("out", (P, B, E), F32, kind="ExternalOutput").ap())
    build(nc, *args)
    r = run_bass_kernel_spmd(nc, [arrays], core_ids=[0])
    return r.results[0]["out"].transpose(1, 0, 2)
```

```python
from contextlib import ExitStack

import numpy as np

import concourse.bass as bass
from concourse import mybir
from concourse.alu_op_type import AluOpType as ALU

ACT = mybir.ActivationFunctionType
AX_X = mybir.AxisListType.X
F32 = mybir.dt.float32
F32R = mybir.dt.float32r
I32 = mybir.dt.int32

P = 128
B = 8
E = 512
C = E // P
T = B * P
NH = 32
G = 8
J = NH // G
HALF = T // 2
TPH = B // 2
MAX_POS = 512
PC = MAX_POS // P
THETA = 10000.0
NE = 16
NX = 18
RG = 4
EPG = NE // RG
SCALE = 1.0 / float(np.sqrt(np.float32(P)))
MASKED = -1.0e9
HUGE = 3.0e38
EPS = 1e-5
OUT_OF_REACH = 1.0e30

EARLY, LATE = range(2)
HALF1 = [("K", 1, 0, 0, EARLY), ("Q", 1, 0, 0, LATE), ("Q", 1, 1, 1, EARLY), ("Q", 1, 2, 1, LATE),
         ("Q", 1, 3, 2, EARLY), ("VT", 1, 0, 2, LATE), ("V", 1, 0, 3, LATE)]
HALF0 = [("K", 0, 0, 4, EARLY), ("Q", 0, 0, 5, EARLY), ("Q", 0, 1, 5, LATE), ("Q", 0, 2, 6, EARLY),
         ("Q", 0, 3, 7, EARLY), ("VT", 0, 0, 8, LATE), ("V", 0, 0, 9, LATE)]
NP0 = len(HALF0)
PROJECTIONS = HALF1 + HALF0
NP = len(PROJECTIONS)
STEPS = B + 2
PROLOGUE_K = [NP0]
PROLOGUE_REST = list(range(NP0 + 1, NP))
TURN_STEP = 7
D2 = P // 2
WEIGHTS = ["k", "q0", "q1", "q2", "q3", "v"]
SPLIT_STEP = [1, 2, 2, 3, 4, 5]
NW = len(WEIGHTS)


def is_roped(p):
    return p[0] in ("Q", "K")


NR0 = sum(map(is_roped, HALF0))
NR = sum(map(is_roped, PROJECTIONS))


def weight_of(kind, j):
    return WEIGHTS.index({"Q": f"q{j}", "K": "k", "VT": "v"}[kind])


def made_before(g, n):
    return g * NP + NP0 + n


def made_in(s, when, last):
    return [n for n in range(NP0 if last else NP) if PROJECTIONS[n][3:] == (s, when)]


def place(kind, h, j=0):
    return next(n for n, p in enumerate(PROJECTIONS) if p[:3] == (kind, h, j))


def build(nc, x, ctx_in, pos, mask, wq, wkv, wo, rw, rb, rbias, w12, w3, b3, rope, iota, ident_in, out):
    with ExitStack() as stack:
        def sb(name, shape, dt=F32):
            return stack.enter_context(nc.sbuf_tensor(f"sb_{name}", shape, dt))

        def sem(name):
            return stack.enter_context(nc.semaphore(f"s_{name}"))

        bank = [stack.enter_context(nc.psum_tensor(f"bank{i}_ps", [P, 512], F32)) for i in range(8)]

        acc = sb("acc", [P, B, E])
        act_hi = sb("act_hi", [P, C, T], F32R)
        act_lo = sb("act_lo", [P, C, T], F32R)
        ctx_hi = sb("ctx_hi", [P, C, T], F32R)
        ctx_lo = sb("ctx_lo", [P, C, T], F32R)
        cap = sb("cap", [P, B, P])
        cos_t = sb("cos_t", [P, T])
        sin_t = sb("sin_t", [P, T])
        q_t = sb("q_t", [P, J, T])
        k_t = sb("k_t", [P, T])
        v_t = sb("v_t", [P, HALF])
        v_hi = sb("v_hi", [P, B, P], F32R)
        v_lo = sb("v_lo", [P, B, P], F32R)
        wq_raw = sb("wq_raw", [P, J, C, P])
        wq_hi = sb("wq_hi", [P, J, C, P], F32R)
        wq_lo = sb("wq_lo", [P, J, C, P], F32R)
        wkv_raw = sb("wkv_raw", [P, 2, C, P])
        wkv_hi = sb("wkv_hi", [P, 2, C, P], F32R)
        wkv_lo = sb("wkv_lo", [P, 2, C, P], F32R)
        wo_raw = sb("wo_raw", [P, J, E])
        wo_hi = sb("wo_hi", [P, J, E], F32R)
        wo_lo = sb("wo_lo", [P, J, E], F32R)
        capped = sb("capped", [P, 2, J, P])
        probs = sb("probs", [P, 2, J, P])
        probs_hi = sb("probs_hi", [P, J * P], F32R)
        probs_lo = sb("probs_lo", [P, J * P], F32R)
        o_hi = sb("o_hi", [P, J, P], F32R)
        o_lo = sb("o_lo", [P, J, P], F32R)
        rope_a = sb("rope_a", [P, 2, HALF])
        rope_b = sb("rope_b", [P, 2, HALF])
        neg_max = sb("neg_max", [P, 2, J])
        row_sum = sb("row_sum", [P, 2, J])
        row_inv = sb("row_inv", [P, 2, J])
        ident = sb("ident", [P, P])
        iota_t = sb("iota_t", [P, PC])
        stats = sb("stats", [P, B, 6])
        mean_var = sb("mean_var", [P, B, 2])
        var_eps = sb("var_eps", [P, B])
        minus_half = sb("minus_half", [P, B])
        rstd = sb("rstd", [P, B])
        tmp8 = sb("tmp8", [P, B])
        rw_hi = sb("rw_hi", [P, C, NE], F32R)
        rw_lo = sb("rw_lo", [P, C, NE], F32R)

        def normed(b):
            return q_t[:, b % TPH, b // TPH * HALF:(b // TPH + 1) * HALF]

        ctx_raw = wq_raw[:, :, :, :].rearrange("p j c n -> p j (c n)")
        ctx_raw2 = wo_raw
        rope_tab = v_t[:, :].rearrange("p (c n) -> p c n", n=P)
        one_hot = rope_a
        pos_f = probs[:, :, :, :].rearrange("p a j n -> p (a j n)")
        pos_i = capped[:, :, :, :].rearrange("p a j n -> p (a j n)").bitcast(I32)
        mask_i = rope_b[:, :, :].rearrange("p a (b k) -> p (a b) k", k=P).bitcast(I32)
        r1, r2, r3, r4 = (probs[:, i // 2, 2 * (i % 2), :].rearrange("p (b e) -> p b e", e=NE) for i in range(4))
        after = wkv_raw[:, :, :, :].rearrange("p a c n -> p (a c n)")
        rw_sb = after[:, 0:C * NE].rearrange("p (c e) -> p c e", c=C)
        rb_sb = after[:, 64:64 + NE]
        rbias_sb = after[:, 96:96 + NE]
        gates = after[:, 256:256 + B * NX].rearrange("p (b e) -> p b e", b=B)
        firsts = after[:, 112:112 + NE]
        s8 = after[:, 400:400 + B]
        cmp8 = after[:, 408:408 + B]
        gmax = after[:, 416:416 + B * RG].rearrange("p (b g) -> p b g", b=B)
        keep = after[:, 448:448 + B * RG].rearrange("p (b g) -> p b g", b=B)
        silu_t = rope_a
        h_t = rope_b
        h_hi = ctx_hi[:, 0:2, 0:HALF]
        h_lo = ctx_lo[:, 0:2, 0:HALF]
        logits_t = cos_t[0:NE, :]
        gates_t = sin_t[0:NE + 1, :]
        b3_sb = v_t[0:NE + 1, :]
        ew_raw, ew_hi, ew_lo = wq_raw, wq_hi, wq_lo
        ew3_raw, ew3_hi, ew3_lo = wo_raw[:, :, :].rearrange("p j e -> p (j e)"), wo_hi, wo_lo

        x_loaded = [sem(f"x_loaded{h}") for h in range(2)]
        ctx_loaded = [sem(f"ctx_loaded{h}") for h in range(2)]
        pos_loaded = sem("pos_loaded")
        mask_loaded = sem("mask_loaded")
        consts_loaded = sem("consts_loaded")
        rope_loaded = sem("rope_loaded")
        router_loaded = sem("router_loaded")
        wq0_loaded = sem("wq0_loaded")
        wqkv_loaded = sem("wqkv_loaded")
        wo_loaded = sem("wo_loaded")
        chain = sem("chain")
        normed_ready = sem("normed_ready")
        turned = sem("turned")
        turned_hi = sem("turned_hi")
        turned_split = sem("turned_split")
        hot_ready = sem("hot_ready")
        hot_used = sem("hot_used")
        b3_loaded = sem("b3_loaded")
        trig_ready = sem("trig_ready")
        cap_ready = sem("cap_ready")
        wqkv_hi = sem("wqkv_hi")
        wqkv_split = sem("wqkv_split")
        wo_hi_done = sem("wo_hi_done")
        wo_split = sem("wo_split")
        proj_ready = sem("proj_ready")
        proj_written = sem("proj_written")
        proj_hi = sem("proj_hi")
        rope_parts = sem("rope_parts")
        scores_ready = sem("scores_ready")
        scores_capped = sem("scores_capped")
        max_ready = sem("max_ready")
        exp_done = sem("exp_done")
        inv_ready = sem("inv_ready")
        probs_ready = sem("probs_ready")
        probs_turned = sem("probs_turned")
        probs_hi_done = sem("probs_hi_done")
        probs_split = sem("probs_split")
        o_ready = sem("o_ready")
        o_hi_done = sem("o_hi_done")
        o_split = sem("o_split")
        out_ready = sem("out_ready")
        out_added = sem("out_added")
        stats_ready = sem("stats_ready")
        logits_ready = sem("logits_ready")
        logits_copied = sem("logits_copied")
        logits_turned = sem("logits_turned")
        logits_read = sem("logits_read")
        route_max = sem("route_max")
        route_exp = sem("route_exp")
        gates_ready = sem("gates_ready")
        gates_turned = sem("gates_turned")
        gates_copied = sem("gates_copied")
        rw_split = sem("rw_split")
        bias_ready = sem("bias_ready")
        bias_added = sem("bias_added")
        ew_loaded = sem("ew_loaded")
        ew3_loaded = sem("ew3_loaded")
        ew_hi_done = sem("ew_hi_done")
        ew_split = sem("ew_split")
        ew3_hi_done = sem("ew3_hi_done")
        ew3_split = sem("ew3_split")
        h1_ready = sem("h1_ready")
        h2_ready = sem("h2_ready")
        silu_done = sem("silu_done")
        h_done = sem("h_done")
        h_hi_done = sem("h_hi_done")
        h_split = sem("h_split")
        y_ready = sem("y_ready")
        y_added = sem("y_added")
        stored = sem("stored")

        def half(h):
            return slice(h * HALF, (h + 1) * HALF)

        def tile_cols(b):
            return slice(b * P, (b + 1) * P)

        def turn_bank(n):
            return bank[n % 2 if 2 * B <= n < 2 * B + TPH else 4 + n % 2]

        def in_step(s):
            return s < B, 1 <= s <= B, 2 <= s <= B + 1

        block = stack.enter_context(nc.Block())

        @block.sync
        def _(sp):
            halves = [slice(0, TPH), slice(TPH, B)]
            sp.dma_start(pos_i, pos).then_inc(pos_loaded, 16)
            sp.dma_start(iota_t[:], iota).then_inc(consts_loaded, 16)
            sp.dma_start(ident[:], ident_in).then_inc(consts_loaded, 16)
            sp.dma_start(rope_tab, rope).then_inc(rope_loaded, 16)
            sp.dma_start(acc[:, halves[0], :], x[:, halves[0], :]).then_inc(x_loaded[0], 16)
            sp.dma_start(ctx_raw, ctx_in[:, halves[0], :]).then_inc(ctx_loaded[0], 16)
            sp.dma_start(wkv_raw[:], wkv[0]).then_inc(wqkv_loaded, 16)
            sp.dma_start(acc[:, halves[1], :], x[:, halves[1], :]).then_inc(x_loaded[1], 16)
            sp.dma_start(ctx_raw2[:], ctx_in[:, halves[1], :]).then_inc(ctx_loaded[1], 16)
            sp.wait_ge(turned, TPH)
            sp.dma_start(wq_raw[:], wq[0]).then_inc(wq0_loaded, 16)
            sp.dma_start(mask_i, mask).then_inc(mask_loaded, 16)
            sp.wait_ge(turned, 3 * TPH)
            sp.dma_start(wo_raw[:], wo[0]).then_inc(wo_loaded, 16)
            with sp.Fori(1, G) as g:
                sp.wait_ge(wqkv_split, g * NW)
                sp.dma_start(wq_raw[:], wq[bass.ds(g, 1)].rearrange("a p j c n -> p (a j) c n")).then_inc(wqkv_loaded, 16)
                sp.dma_start(wkv_raw[:], wkv[bass.ds(g, 1)].rearrange("a p j c n -> p (a j) c n")).then_inc(wqkv_loaded, 16)
                sp.wait_ge(wo_split, g * J)
                sp.dma_start(wo_raw[:], wo[bass.ds(g, 1)].rearrange("a p j n -> p (a j) n")).then_inc(wo_loaded, 16)
            sp.wait_ge(wqkv_split, G * NW)
            sp.dma_start(rw_sb, rw).then_inc(router_loaded, 16)
            sp.dma_start(rb_sb, rb).then_inc(router_loaded, 16)
            sp.dma_start(rbias_sb, rbias).then_inc(router_loaded, 16)
            sp.dma_start(ew_raw[:, 0:2], w12[0]).then_inc(ew_loaded, 16)
            sp.wait_ge(wo_split, G * J)
            sp.dma_start(ew3_raw[:, 0:E + 2], w3[0]).then_inc(ew3_loaded, 16)
            sp.wait_ge(proj_ready, G * NP)
            sp.dma_start(b3_sb, b3).then_inc(b3_loaded, 16)
            with sp.Fori(1, NX) as e:
                sp.wait_ge(ew_split, e * 2)
                sp.dma_start(ew_raw[:, 0:2], w12[bass.ds(e, 1)].rearrange("a p j c n -> p (a j) c n")).then_inc(ew_loaded, 16)
                sp.wait_ge(ew3_split, e)
                sp.wait_ge(h_done, e * 2)
                sp.dma_start(ew3_raw[:, 0:E + 2], w3[bass.ds(e, 1)].rearrange("a p n -> p (a n)")).then_inc(ew3_loaded, 16)
            for b in range(B):
                sp.wait_ge(y_added, (NX - 1) * B + b + 1)
                sp.dma_start(out[:, b, :], acc[:, b, :]).then_inc(stored, 16)
            sp.wait_ge(stored, B * 16)

        @block.tensor
        def _(pe):
            def product(out_ap, st_hi, st_lo, mv_hi, mv_lo, first, last):
                pe.matmul(out_ap, st_lo, mv_hi, start=first, stop=False)
                pe.matmul(out_ap, st_hi, mv_lo, start=False, stop=False)
                return pe.matmul(out_ap, st_hi, mv_hi, start=False, stop=last)

            def project(n, g):
                kind, h, j = PROJECTIONS[n][:3]
                of = g + 1 - h
                dst = bank[(NP0 + n) % 2]
                if not (isinstance(g, int) and made_before(g, n) < 2):
                    pe.wait_ge(proj_written, made_before(g, n) - 1)
                if kind == "V":
                    pe.wait_ge(proj_written, made_before(g, place("VT", h)) + 1)
                    for i in range(TPH):
                        ins = pe.transpose(dst[:, tile_cols(i)], v_t[:, tile_cols(i)], ident[:, :])
                    ins.then_inc(proj_ready, 1)
                    return
                if h == 0:
                    pe.wait_ge(wqkv_split, of * NW + weight_of(kind, j) + 1)
                w_hi, w_lo = (wq_hi, wq_lo) if kind == "Q" else (wkv_hi, wkv_lo)
                slot = {"Q": j, "K": 0, "VT": 1}[kind]
                m_hi, m_lo = (act_hi, act_lo) if kind == "Q" else (ctx_hi, ctx_lo)
                for c in range(C):
                    ins = product(dst[:, :], w_hi[:, slot, c, :], w_lo[:, slot, c, :],
                                  m_hi[:, c, half(h)], m_lo[:, c, half(h)], c == 0, c == C - 1)
                ins.then_inc(proj_ready, 1)

            def turn_tile(src, n):
                if n not in (0, 1, 2 * B, 2 * B + 1, 2 * B + TPH, 2 * B + TPH + 1):
                    pe.wait_ge(turned_split, n - 1)
                for c in range(C):
                    ins = pe.transpose(turn_bank(n)[:, tile_cols(c)], src[:, c * P:(c + 1) * P], ident[:, :])
                ins.then_inc(turned, 1)

            def attend(g, last):
                for s in range(STEPS):
                    a, t, w = in_step(s)
                    if a:
                        if s == 0:
                            pe.wait_ge(proj_written, made_before(g, 0))
                        if s == TPH:
                            pe.wait_ge(proj_written, made_before(g, place("Q", 1, J - 1)) + 1)
                        if not (isinstance(g, int) and g == 0 and s < 2):
                            pe.wait_ge(scores_capped, g * B + s - 1)
                        for j in range(J):
                            ins = pe.matmul(bank[2 + s % 2][:, tile_cols(j)], q_t[:, j, tile_cols(s)],
                                            k_t[:, tile_cols(s)], start=True, stop=True)
                        ins.then_inc(scores_ready, 1)
                    if t:
                        b = s - 1
                        pe.wait_ge(probs_ready, g * B + b + 1)
                        for j in range(J):
                            ins = pe.transpose(bank[4][:, tile_cols(j)], probs[:, b % 2, j, :], ident[:, :])
                        ins.then_inc(probs_turned, 1)
                    for n in made_in(s, EARLY, last):
                        project(n, g)
                    if w:
                        b = s - 2
                        pe.wait_ge(o_split, g * B + b + 1)
                        if b == 0:
                            pe.wait_ge(wo_split, g * J + J)
                        if not (isinstance(g, int) and g == 0 and b < 2):
                            pe.wait_ge(out_added, g * B + b - 1)
                        for j in range(J):
                            ins = product(bank[6 + b % 2][:, :], o_hi[:, j, :], o_lo[:, j, :],
                                          wo_hi[:, j, :], wo_lo[:, j, :], j == 0, j == J - 1)
                        ins.then_inc(out_ready, 1)
                    if t:
                        b = s - 1
                        if b == TPH:
                            pe.wait_ge(proj_written, made_before(g, place("V", 1)) + 1)
                        pe.wait_ge(probs_split, g * B + b + 1)
                        product(bank[5][:, :], v_hi[:, b, :], v_lo[:, b, :], probs_hi[:, :], probs_lo[:, :],
                                True, True).then_inc(o_ready, 1)
                    for n in made_in(s, LATE, last):
                        project(n, g)
                    if last and s == TURN_STEP:
                        for b in range(TPH):
                            pe.wait_ge(normed_ready, B + b + 1)
                            turn_tile(normed(b), 2 * B + b)

            def expert_h(e, h):
                if h == 0:
                    pe.wait_ge(ew_split, e * 2 + 2)
                if not (isinstance(e, int) and e == 0):
                    pe.wait_ge(h_done, e * 2 + h - 1)
                for a, ready in ((0, h1_ready), (1, h2_ready)):
                    for c in range(C):
                        ins = product(bank[2 * h + a][:, :], ew_hi[:, a, c, :], ew_lo[:, a, c, :],
                                      act_hi[:, c, half(h)], act_lo[:, c, half(h)], c == 0, c == C - 1)
                    ins.then_inc(ready, 1)

            def expert_y(e, b):
                if b == 0:
                    pe.wait_ge(ew3_split, e + 1)
                if b % TPH == 0:
                    pe.wait_ge(h_split, e * 2 + b // TPH + 1)
                if not (isinstance(e, int) and e == 0 and b < 4):
                    pe.wait_ge(y_added, e * B + b - 3)
                product(bank[4 + b % 4][:, :], h_hi[:, b // TPH, tile_cols(b % TPH)], h_lo[:, b // TPH, tile_cols(b % TPH)],
                        ew3_hi[:, 0, :], ew3_lo[:, 0, :], True, True).then_inc(y_ready, 1)

            pe.wait_ge(consts_loaded, 32)
            pe.wait_ge(rope_loaded, 16)
            for h in range(2):
                for c in range(PC):
                    pe.wait_ge(hot_ready, h * PC + c + 1)
                    pe.matmul(bank[2 + h][:, :], rope_tab[:, c, :], one_hot[:, c % 2, :],
                              start=(c == 0), stop=(c == PC - 1)).then_inc(hot_used, 1)
            pe.wait_ge(ctx_loaded[0], 16)
            for b in range(TPH):
                turn_tile(ctx_raw[:, b, :], b)
            for b in range(TPH):
                pe.wait_ge(normed_ready, b + 1)
                turn_tile(normed(b), TPH + b)
            pe.wait_ge(turned_split, TPH)
            for n in PROLOGUE_K:
                project(n, -1)
            pe.wait_ge(ctx_loaded[1], 16)
            for b in range(TPH):
                turn_tile(ctx_raw2[:, b, :], 2 * TPH + b)
            for b in range(TPH):
                pe.wait_ge(normed_ready, TPH + b + 1)
                turn_tile(normed(TPH + b), 3 * TPH + b)
            for n in PROLOGUE_REST:
                project(n, -1)
            pe.wait_ge(turned_split, 2 * B)
            pe.wait_ge(trig_ready, 8)
            attend(0, False)
            with pe.Fori(1, G - 1) as g:
                attend(g, False)
            attend(G - 1, True)

            pe.wait_ge(turned_split, 2 * B + TPH)
            expert_h(0, 0)
            for b in range(TPH, B):
                pe.wait_ge(normed_ready, B + b + 1)
                turn_tile(normed(b), 2 * B + b)
            pe.wait_ge(turned_split, 3 * B)
            pe.wait_ge(rw_split, 1)
            for h in range(2):
                for c in range(C):
                    ins = product(bank[6 + h][0:NE, :], rw_hi[:, c, :], rw_lo[:, c, :], act_hi[:, c, half(h)],
                                  act_lo[:, c, half(h)], c == 0, c == C - 1)
            ins.then_inc(logits_ready, 1)
            expert_h(0, 1)
            pe.wait_ge(logits_copied, 2)
            for b in range(B):
                ins = pe.transpose(bank[7][:, b * NE:(b + 1) * NE], logits_t[:, tile_cols(b)], ident[0:NE, 0:NE])
            ins.then_inc(logits_turned, 1)
            for b in range(B):
                if b == 3:
                    pe.wait_ge(logits_read, 1)
                expert_y(0, b)

            def expert(e):
                expert_h(e, 0)
                expert_h(e, 1)
                for b in range(B):
                    expert_y(e, b)

            expert(1)
            pe.wait_ge(gates_ready, 1)
            pe.wait_ge(y_added, 2 * B)
            for b in range(B):
                ins = pe.transpose(bank[4 + b // TPH][0:NE + 1, tile_cols(b % TPH)], gates[:, b, 1:NX], ident[:, :])
            ins.then_inc(gates_turned, 1)
            pe.wait_ge(gates_copied, 1)
            pe.wait_ge(b3_loaded, 16)
            for b in range(B):
                if b >= 2:
                    pe.wait_ge(bias_added, b - 1)
                pe.matmul(bank[6 + b % 2][:, :], gates_t[:, tile_cols(b)], b3_sb, start=True, stop=True).then_inc(bias_ready, 1)
            pe.wait_ge(bias_added, B)
            with pe.Fori(2, NX) as e:
                expert(e)

        @block.scalar
        def _(act):
            def turn_hi(n, dst):
                act.wait_ge(turned, n + 1)
                nc.scalar.copy(dst, turn_bank(n)[:, :].rearrange("p (c t) -> p c t", c=C)).then_inc(turned_hi, 1)

            def split_qkv(i, g):
                w = WEIGHTS[i]
                if w[0] == "q":
                    src, dst = wq_raw[:, int(w[1])], wq_hi[:, int(w[1])]
                else:
                    src, dst = wkv_raw[:, "kv".index(w)], wkv_hi[:, "kv".index(w)]
                if isinstance(g, int) and g == 0:
                    if i == 0:
                        act.wait_ge(wqkv_loaded, 16)
                    if i == 1:
                        act.wait_ge(wq0_loaded, 16)
                else:
                    if i == 0:
                        act.wait_ge(wqkv_loaded, g * 32 + 16)
                    kind = {"q": "Q", "k": "K", "v": "VT"}[w[0]]
                    act.wait_ge(proj_ready, made_before(g - 1, place(kind, 1, int(w[1]) if w[0] == "q" else 0)) + 1)
                nc.scalar.copy(dst, src).then_inc(wqkv_hi, 1)

            def split_wo(j, g):
                if j == 0:
                    act.wait_ge(wo_loaded, g * 16 + 16)
                    if not (isinstance(g, int) and g == 0):
                        act.wait_ge(out_ready, g * B)
                nc.scalar.copy(wo_hi[:, j, :], wo_raw[:, j, :]).then_inc(wo_hi_done, 1)

            def project_hi(n, g):
                kind, h, j = PROJECTIONS[n][:3]
                if kind == "V":
                    act.wait_ge(proj_ready, made_before(g, n) + 1)
                    nc.scalar.copy(v_hi[:, h * TPH:(h + 1) * TPH, :],
                                   bank[(NP0 + n) % 2][:, :].rearrange("p (b d) -> p b d", d=P)).then_inc(proj_hi, 1)

            def expert_w(e):
                act.wait_ge(ew_loaded, e * 16 + 16)
                if isinstance(e, int) and e == 0:
                    act.wait_ge(proj_ready, G * NP)
                else:
                    act.wait_ge(h2_ready, e * 2)
                for a in range(2):
                    nc.scalar.copy(ew_hi[:, a], ew_raw[:, a]).then_inc(ew_hi_done, 1)

            def attend(g, last, first=False):
                for s in range(STEPS):
                    a, t, w = in_step(s)
                    if t:
                        act.wait_ge(probs_turned, g * B + s)
                        nc.scalar.copy(probs_hi[:, :], bank[4][:, :]).then_inc(probs_hi_done, 1)
                    if a:
                        act.wait_ge(max_ready, g * B + s + 1)
                        for j in range(J):
                            ins = nc.scalar.activation(probs[:, s % 2, j, :], capped[:, s % 2, j, :], ACT.Exp,
                                                       bias=neg_max[:, s % 2, j:j + 1], scale=1.0,
                                                       accum_out=row_sum[:, s % 2, j:j + 1])
                        ins.then_inc(exp_done, 1)
                    if t:
                        act.wait_ge(o_ready, g * B + s)
                        nc.scalar.copy(o_hi[:, :, :], bank[5][:, :].rearrange("p (j t) -> p j t", j=J)).then_inc(o_hi_done, 1)
                    if not last:
                        for i in range(NW):
                            if SPLIT_STEP[i] == s:
                                split_qkv(i, g + 1)
                    if s == 0 and not first:
                        for j in range(J):
                            split_wo(j, g)
                    for n in made_in(s, EARLY, last) + made_in(s, LATE, last):
                        project_hi(n, g)
                    if last and s == TURN_STEP - 1:
                        expert_w(0)
                    if last and s == TURN_STEP:
                        for b in range(TPH):
                            turn_hi(2 * B + b, act_hi[:, :, tile_cols(b)])

            for n, dst in ((0, ctx_hi), (TPH, act_hi)):
                if n == 0:
                    for h in range(2):
                        act.wait_ge(hot_used, (h + 1) * PC)
                        nc.scalar.copy(cos_t[0:D2, half(h)], bank[2 + h][0:D2, :]).then_inc(trig_ready, 1)
                        nc.scalar.copy(cos_t[D2:P, half(h)], bank[2 + h][0:D2, :]).then_inc(trig_ready, 1)
                        nc.scalar.copy(sin_t[0:D2, half(h)], bank[2 + h][D2:P, :]).then_inc(trig_ready, 1)
                        nc.scalar.mul(sin_t[D2:P, half(h)], bank[2 + h][D2:P, :], -1.0).then_inc(trig_ready, 1)
                for b in range(TPH):
                    turn_hi(n + b, dst[:, :, tile_cols(b)])
                if n == 0:
                    split_qkv(0, 0)
            for i in range(1, NW):
                split_qkv(i, 0)
            for b in range(TPH, B):
                turn_hi(TPH + b, ctx_hi[:, :, tile_cols(b)])
            for b in range(TPH, B):
                turn_hi(2 * TPH + b, act_hi[:, :, tile_cols(b)])
            for n in range(NP0, NP):
                project_hi(n, -1)
            for j in range(J):
                split_wo(j, 0)
            attend(0, False, True)
            with act.Fori(1, G - 1) as g:
                attend(g, False)
            attend(G - 1, True)

            def expert_w3(e):
                act.wait_ge(ew3_loaded, e * 16 + 16)
                if isinstance(e, int) and e == 0:
                    act.wait_ge(out_ready, G * B)
                else:
                    act.wait_ge(y_ready, e * B)
                nc.scalar.copy(ew3_hi[:, 0, :], ew3_raw[:, 0:E]).then_inc(ew3_hi_done, 1)

            def expert_inner(e, h):
                act.wait_ge(h1_ready, e * 2 + h + 1)
                nc.scalar.activation(silu_t[:, h, :], bank[2 * h][:, :], ACT.Silu,
                                     bias=ew3_raw[:, E:E + 1], scale=1.0).then_inc(silu_done, 1)
                act.wait_ge(h_done, e * 2 + h + 1)
                nc.scalar.copy(h_hi[:, h, :], h_t[:, h, :]).then_inc(h_hi_done, 1)

            def expert(e):
                expert_w3(e)
                for h in range(2):
                    expert_inner(e, h)

            expert_w3(0)
            expert_inner(0, 0)
            for b in range(TPH, B):
                turn_hi(2 * B + b, act_hi[:, :, tile_cols(b)])
            act.wait_ge(logits_ready, 1)
            for h in range(2):
                nc.scalar.copy(logits_t[:, half(h)], bank[6 + h][0:NE, :]).then_inc(logits_copied, 1)
            expert_inner(0, 1)
            expert_w(1)
            act.wait_ge(route_max, 1)
            nc.scalar.activation(r2, r1, ACT.Exp).then_inc(route_exp, 1)
            with act.Fori(1, NX - 1) as e:
                expert(e)
                expert_w(e + 1)
            expert(NX - 1)

        @block.gpsimd
        def _(pool):
            def low(dst, raw, hi):
                return nc.gpsimd.tensor_tensor(dst, raw, hi.bitcast(F32), ALU.subtract)

            def split_qkv(g):
                for i, w in enumerate(WEIGHTS):
                    pool.wait_ge(wqkv_hi, g * NW + i + 1)
                    if w[0] == "q":
                        j = int(w[1])
                        ins = low(wq_lo[:, j], wq_raw[:, j], wq_hi[:, j])
                    else:
                        a = "kv".index(w)
                        ins = low(wkv_lo[:, a], wkv_raw[:, a], wkv_hi[:, a])
                    ins.then_inc(wqkv_split, 1)

            def split_wo(g):
                for j in range(J):
                    pool.wait_ge(wo_hi_done, g * J + j + 1)
                    low(wo_lo[:, j, :], wo_raw[:, j, :], wo_hi[:, j, :]).then_inc(wo_split, 1)

            split_qkv(0)
            split_wo(0)
            with pool.Fori(1, G) as g:
                split_qkv(g)
                split_wo(g)
            with pool.Fori(0, NX) as e:
                for a in range(2):
                    pool.wait_ge(ew_hi_done, e * 2 + a + 1)
                    low(ew_lo[:, a], ew_raw[:, a], ew_hi[:, a]).then_inc(ew_split, 1)
                pool.wait_ge(ew3_hi_done, e + 1)
                low(ew3_lo[:, 0, :], ew3_raw[:, 0:E], ew3_hi[:, 0, :]).then_inc(ew3_split, 1)

        @block.vector
        def _(dve):
            count = [0]

            def link(ins):
                count[0] += 1
                ins.then_inc(chain, 1)
                dve.wait_ge(chain, count[0])

            def tile_stats(b, done):
                nc.vector.bn_stats(stats[:, b, :], acc[:, b, :]).then_inc(stats_ready, 1)
                dve.wait_ge(stats_ready, 2 * done + 1)
                nc.vector.bn_aggr(mean_var[:, b, :], stats[:, b, :]).then_inc(stats_ready, 1)

            def normalise(h, done):
                cols = slice(h * TPH, (h + 1) * TPH)
                y, v, m = rstd[:, cols], var_eps[:, cols], minus_half[:, cols]
                dve.wait_ge(stats_ready, 2 * done)
                link(nc.vector.tensor_scalar(v, mean_var[:, cols, 1], EPS, None, ALU.add))
                link(nc.vector.tensor_scalar(m, v, -0.5, None, ALU.mult))
                link(nc.vector.tensor_scalar(y.bitcast(I32), v.bitcast(I32), 1, None, ALU.logical_shift_right))
                link(nc.vector.tensor_scalar(y.bitcast(I32), y.bitcast(I32), -1.0, float(0x5F3759DF), ALU.mult, ALU.add))
                for _ in range(4):
                    link(nc.vector.tensor_tensor(tmp8[:, cols], y, y, ALU.mult))
                    link(nc.vector.tensor_tensor(tmp8[:, cols], tmp8[:, cols], m, ALU.mult))
                    link(nc.vector.scalar_tensor_tensor(out=y, in0=tmp8[:, cols], scalar=1.5, in1=y, op0=ALU.add, op1=ALU.mult))
                for b in range(h * TPH, (h + 1) * TPH):
                    nc.vector.tensor_scalar(normed(b), acc[:, b, :], mean_var[:, b, 0:1], rstd[:, b:b + 1],
                                            ALU.subtract, ALU.mult).then_inc(normed_ready, 1)

            def turn_lo(n, hi, lo):
                dve.wait_ge(turned_hi, n + 1)
                nc.vector.tensor_tensor(lo, turn_bank(n)[:, :].rearrange("p (c t) -> p c t", c=C), hi.bitcast(F32),
                                        ALU.subtract).then_inc(turned_split, 1)

            def project_out(n, g):
                kind, h, j = PROJECTIONS[n][:3]
                dve.wait_ge(proj_ready, made_before(g, n) + 1)
                src = bank[(NP0 + n) % 2]
                if kind == "VT":
                    nc.vector.tensor_copy(v_t[:, :], src[:, :]).then_inc(proj_written, 1)
                elif kind == "V":
                    dve.wait_ge(proj_hi, g * 2 + 3 - h)
                    tiles = slice(h * TPH, (h + 1) * TPH)
                    nc.vector.tensor_tensor(v_lo[:, tiles, :], src[:, :].rearrange("p (b d) -> p b d", d=P),
                                            v_hi[:, tiles, :].bitcast(F32), ALU.subtract).then_inc(proj_written, 1)
                else:
                    before = NR0 + sum(map(is_roped, PROJECTIONS[:n]))
                    r = before % 2
                    nc.vector.tensor_tensor(rope_a[:, r, :], src[:, :], cos_t[:, half(h)], ALU.mult)
                    nc.vector.tensor_tensor(rope_b[D2:P, r, :], src[0:D2, :], sin_t[0:D2, half(h)], ALU.mult)
                    nc.vector.tensor_tensor(rope_b[0:D2, r, :], src[D2:P, :], sin_t[D2:P, half(h)],
                                            ALU.mult).then_inc(rope_parts, 1)
                    dve.wait_ge(rope_parts, g * NR + before + 1)
                    dst = q_t[:, j, half(h)] if kind == "Q" else k_t[:, half(h)]
                    nc.vector.tensor_tensor(dst, rope_a[:, r, :], rope_b[:, r, :], ALU.add).then_inc(proj_written, 1)

            def attend(g, last):
                for s in range(STEPS):
                    a, t, w = in_step(s)
                    if a:
                        dve.wait_ge(scores_ready, g * B + s + 1)
                        nc.vector.scalar_tensor_tensor(
                            out=capped[:, s % 2, :, :], in0=bank[2 + s % 2][:, :].rearrange("p (j k) -> p j k", j=J),
                            scalar=SCALE, in1=cap[:, s:s + 1, :].to_broadcast([P, J, P]), op0=ALU.mult,
                            op1=ALU.min).then_inc(scores_capped, 1)
                        dve.wait_ge(scores_capped, g * B + s + 1)
                        nc.vector.tensor_reduce(neg_max[:, s % 2, :], capped[:, s % 2, :, :], AX_X, ALU.max,
                                                negate=True).then_inc(max_ready, 1)
                    if t:
                        dve.wait_ge(probs_hi_done, g * B + s)
                        nc.vector.tensor_tensor(probs_lo[:, :], bank[4][:, :], probs_hi[:, :].bitcast(F32),
                                                ALU.subtract).then_inc(probs_split, 1)
                    if s > 0:
                        for n in made_in(s - 1, LATE, last):
                            project_out(n, g)
                    if a:
                        dve.wait_ge(exp_done, g * B + s + 1)
                        nc.vector.reciprocal(row_inv[:, s % 2, :], row_sum[:, s % 2, :]).then_inc(inv_ready, 1)
                        dve.wait_ge(inv_ready, g * B + s + 1)
                        nc.vector.tensor_tensor(probs[:, s % 2, :, :], probs[:, s % 2, :, :],
                                                row_inv[:, s % 2, :].unsqueeze(2).to_broadcast([P, J, P]),
                                                ALU.mult).then_inc(probs_ready, 1)
                    for n in made_in(s, EARLY, last):
                        project_out(n, g)
                    if w:
                        b = s - 2
                        dve.wait_ge(out_ready, g * B + b + 1)
                        nc.vector.tensor_tensor(acc[:, b, :], acc[:, b, :], bank[6 + b % 2][:, :],
                                                ALU.add).then_inc(out_added, 1)
                    if t:
                        dve.wait_ge(o_hi_done, g * B + s)
                        nc.vector.tensor_tensor(o_lo[:, :, :], bank[5][:, :].rearrange("p (j t) -> p j t", j=J),
                                                o_hi[:, :, :].bitcast(F32), ALU.subtract).then_inc(o_split, 1)
                    if last and w:
                        dve.wait_ge(out_added, g * B + s - 1)
                        tile_stats(s - 2, B + s - 2)
                    if s == STEPS - 1:
                        for n in made_in(s, LATE, last):
                            project_out(n, g)
                    if last and s == TURN_STEP - 1:
                        normalise(0, B + TPH)
                    if last and s == TURN_STEP:
                        for b in range(TPH):
                            turn_lo(2 * B + b, act_hi[:, :, tile_cols(b)], act_lo[:, :, tile_cols(b)])

            def expert_inner(e, h):
                dve.wait_ge(h2_ready, e * 2 + h + 1)
                dve.wait_ge(silu_done, e * 2 + h + 1)
                nc.vector.scalar_tensor_tensor(out=h_t[:, h, :], in0=bank[2 * h + 1][:, :],
                                               scalar=ew3_raw[:, E + 1:E + 2], in1=silu_t[:, h, :],
                                               op0=ALU.add, op1=ALU.mult).then_inc(h_done, 1)
                dve.wait_ge(h_hi_done, e * 2 + h + 1)
                nc.vector.tensor_tensor(h_lo[:, h, :], h_t[:, h, :], h_hi[:, h, :].bitcast(F32),
                                        ALU.subtract).then_inc(h_split, 1)

            def expert_added(e):
                for b in range(B):
                    dve.wait_ge(y_ready, e * B + b + 1)
                    nc.vector.scalar_tensor_tensor(out=acc[:, b, :], in0=bank[4 + b % 4][:, :],
                                                   scalar=gates[:, b, bass.ds(e, 1)], in1=acc[:, b, :],
                                                   op0=ALU.mult, op1=ALU.add).then_inc(y_added, 1)

            dve.wait_ge(pos_loaded, 16)
            dve.wait_ge(consts_loaded, 32)
            link(nc.vector.tensor_copy(pos_f, pos_i))
            for h in range(2):
                for c in range(PC):
                    n = h * PC + c
                    if n >= 2:
                        dve.wait_ge(hot_used, n - 1)
                    nc.vector.tensor_scalar(one_hot[:, c % 2, :], pos_f[:, half(h)], iota_t[:, c:c + 1], None,
                                            ALU.is_equal).then_inc(hot_ready, 1)
            dve.wait_ge(x_loaded[0], 16)
            for b in range(TPH):
                tile_stats(b, b)
            normalise(0, TPH)
            for b in range(TPH):
                turn_lo(b, ctx_hi[:, :, tile_cols(b)], ctx_lo[:, :, tile_cols(b)])
            for b in range(TPH):
                turn_lo(TPH + b, act_hi[:, :, tile_cols(b)], act_lo[:, :, tile_cols(b)])
            dve.wait_ge(mask_loaded, 16)
            link(nc.vector.tensor_scalar(cap[:, :, :], mask_i, 0.0, HUGE, ALU.not_equal, ALU.mult))
            link(nc.vector.tensor_scalar(cap[:, :, :], cap[:, :, :], MASKED, None, ALU.add))
            dve.wait_ge(x_loaded[1], 16)
            for b in range(TPH, B):
                tile_stats(b, b)
            normalise(1, B)
            dve.wait_ge(trig_ready, 8)
            for n in PROLOGUE_K:
                project_out(n, -1)
            for b in range(TPH, B):
                turn_lo(TPH + b, ctx_hi[:, :, tile_cols(b)], ctx_lo[:, :, tile_cols(b)])
            for b in range(TPH, B):
                turn_lo(2 * TPH + b, act_hi[:, :, tile_cols(b)], act_lo[:, :, tile_cols(b)])
            for n in PROLOGUE_REST:
                project_out(n, -1)
            attend(0, False)
            with dve.Fori(1, G - 1) as g:
                attend(g, False)
            attend(G - 1, True)

            dve.wait_ge(router_loaded, 48)
            link(nc.vector.tensor_copy(rw_hi[:, :, :], rw_sb))
            nc.vector.tensor_tensor(rw_lo[:, :, :], rw_sb, rw_hi[:, :, :].bitcast(F32),
                                    ALU.subtract).then_inc(rw_split, 1)
            normalise(1, 2 * B)
            expert_inner(0, 0)
            for b in range(TPH, B):
                turn_lo(2 * B + b, act_hi[:, :, tile_cols(b)], act_lo[:, :, tile_cols(b)])
            expert_inner(0, 1)

            link(nc.vector.memset(gates[:, :, 0:2], 1.0))
            def over(ap, n):
                return ap.unsqueeze(2).to_broadcast([P, B, n])

            dve.wait_ge(logits_turned, 1)
            logits = bank[7][:, 0:B * NE].rearrange("p (b e) -> p b e", e=NE)
            bias_b = rb_sb.unsqueeze(1).to_broadcast([P, B, NE])
            nc.vector.tensor_tensor(r3, logits, bias_b, ALU.add).then_inc(logits_read, 1)
            dve.wait_ge(logits_read, 1)
            link(nc.vector.tensor_reduce(s8, r3, AX_X, ALU.max))
            nc.vector.tensor_tensor(r1, r3, over(s8[:, :], NE), ALU.subtract).then_inc(route_max, 1)
            expert_added(0)
            dve.wait_ge(route_exp, 1)
            link(nc.vector.reduce_sum(s8, r2, AX_X))
            link(nc.vector.reciprocal(tmp8[:], s8))
            link(nc.vector.tensor_tensor(r1, r2, over(tmp8[:, :], NE), ALU.mult))
            link(nc.vector.tensor_tensor(r1, r1, rbias_sb.unsqueeze(1).to_broadcast([P, B, NE]), ALU.add))
            link(nc.vector.tensor_reduce(gmax, r1.rearrange("p b (g e) -> p b g e", e=EPG), AX_X, ALU.max))
            for i in range(RG):
                link(nc.vector.memset(keep[:, :, i], 0.0))
                for k in range(RG):
                    if k != i:
                        link(nc.vector.tensor_tensor(cmp8[:, :], gmax[:, :, k], gmax[:, :, i],
                                                     ALU.is_ge if k < i else ALU.is_gt))
                        link(nc.vector.tensor_tensor(keep[:, :, i], keep[:, :, i], cmp8[:, :], ALU.add))
            link(nc.vector.tensor_scalar(keep, keep, 1.5, None, ALU.is_lt))
            keep_e = keep[:, :, :].unsqueeze(3).to_broadcast([P, B, RG, EPG])

            def v4_of(r):
                return r.rearrange("p b (g e) -> p b g e", e=EPG)

            link(nc.vector.tensor_tensor(v4_of(r3), v4_of(r1), keep_e, ALU.mult))
            link(nc.vector.tensor_scalar(keep, keep, 1.0, OUT_OF_REACH, ALU.subtract, ALU.mult))
            link(nc.vector.tensor_tensor(v4_of(r3), v4_of(r3), keep_e, ALU.add))
            for e in range(NE):
                last = nc.vector.memset(firsts[:, e:e + 1], float(NE - e))
            link(last)
            link(nc.vector.memset(gates[:, :, 2:NX], 0.0))
            for k in range(2):
                link(nc.vector.tensor_reduce(s8, r3, AX_X, ALU.max))
                link(nc.vector.tensor_tensor(r2, r3, over(s8[:, :], NE), ALU.is_equal))
                link(nc.vector.tensor_tensor(r2, r2, firsts[:, :].unsqueeze(1).to_broadcast([P, B, NE]), ALU.mult))
                link(nc.vector.tensor_reduce(s8, r2, AX_X, ALU.max))
                link(nc.vector.tensor_tensor(r2, r2, over(s8[:, :], NE), ALU.is_equal))
                if k == 0:
                    link(nc.vector.tensor_copy(r4, r2))
                    link(nc.vector.scalar_tensor_tensor(out=r3, in0=r2, scalar=-HUGE, in1=r3, op0=ALU.mult, op1=ALU.add))
                else:
                    link(nc.vector.tensor_tensor(r4, r4, r2, ALU.add))
            nc.vector.tensor_tensor(gates[:, :, 2:NX], r1, r4, ALU.mult).then_inc(gates_ready, 1)

            expert_inner(1, 0)
            expert_inner(1, 1)
            expert_added(1)
            dve.wait_ge(gates_turned, 1)
            for h in range(2):
                last = nc.vector.tensor_copy(gates_t[:, half(h)], bank[4 + h][0:NE + 1, :])
            last.then_inc(gates_copied, 1)
            for b in range(B):
                dve.wait_ge(bias_ready, b + 1)
                nc.vector.tensor_tensor(acc[:, b, :], acc[:, b, :], bank[6 + b % 2][:, :], ALU.add).then_inc(bias_added, 1)
            dve.wait_ge(bias_added, B)
            with dve.Fori(2, NX) as e:
                for h in range(2):
                    expert_inner(e, h)
                expert_added(e)


def _rope_table():
    inv = (np.float32(1.0) / np.power(np.float32(THETA), np.arange(0, P, 2, dtype=np.float32) / np.float32(P))).astype(np.float32)
    f = np.arange(MAX_POS, dtype=np.float32)[:, None] * inv[None, :]
    tab = np.concatenate([np.cos(f), np.sin(f)], 1).astype(np.float32)
    return np.ascontiguousarray(tab.reshape(PC, P, P).transpose(1, 0, 2))


def kernel(x, ctx_4096, pos_BxS2, mask_BxSxS2_ik0, L0_xattn_Wq, L0_xattn_Wk, L0_xattn_Wv, L0_xattn_Wo,
           L0_ffn_router_w, L0_ffn_router_b, L0_ffn_router_bias, L0_ffn_ew1, L0_ffn_eb1, L0_ffn_ew2, L0_ffn_eb2,
           L0_ffn_ew3, L0_ffn_eb3, L0_ffn_sw1, L0_ffn_sb1, L0_ffn_sw2, L0_ffn_sb2, L0_ffn_sw3, L0_ffn_sb3):
    import concourse.bacc as bacc
    from concourse.bass_utils import run_bass_kernel_spmd

    a = np.asarray

    def by_expert(routed, shared):
        both = np.concatenate([a(shared).reshape(E, 2, P).transpose(1, 0, 2), a(routed)])
        return both.reshape(NX, C, P, P).transpose(0, 2, 1, 3)

    wk, wv = (a(w).reshape(C, P, G, P).transpose(2, 1, 0, 3) for w in (L0_xattn_Wk, L0_xattn_Wv))
    arrays = {
        "x": a(x).transpose(1, 0, 2),
        "ctx_in": a(ctx_4096).transpose(1, 0, 2),
        "pos": np.broadcast_to(a(pos_BxS2).reshape(1, T), (P, T)),
        "mask": a(mask_BxSxS2_ik0).transpose(1, 0, 2),
        "wq": a(L0_xattn_Wq).reshape(C, P, G, J, P).transpose(2, 1, 3, 0, 4),
        "wkv": np.stack([wk, wv], 2),
        "wo": a(L0_xattn_Wo).reshape(G, J, P, E).transpose(0, 2, 1, 3),
        "rw": a(L0_ffn_router_w).reshape(C, P, NE).transpose(1, 0, 2),
        "rb": np.broadcast_to(a(L0_ffn_router_b), (P, NE)),
        "rbias": np.broadcast_to(a(L0_ffn_router_bias), (P, NE)),
        "w12": np.stack([by_expert(L0_ffn_ew1, L0_ffn_sw1), by_expert(L0_ffn_ew2, L0_ffn_sw2)], 2),
        "w3": np.concatenate([
            np.concatenate([a(L0_ffn_sw3).reshape(2, P, E), a(L0_ffn_sb1).reshape(2, P, 1), a(L0_ffn_sb2).reshape(2, P, 1)], 2),
            np.concatenate([a(L0_ffn_ew3), a(L0_ffn_eb1)[:, :, None], a(L0_ffn_eb2)[:, :, None]], 2),
        ]),
        "b3": np.concatenate([a(L0_ffn_sb3).reshape(1, E), a(L0_ffn_eb3)]),
        "rope": _rope_table(),
        "iota": (np.arange(P)[:, None] + P * np.arange(PC)[None, :]).astype(np.float32),
        "ident": np.eye(P, dtype=np.float32),
    }
    nc = bacc.Bacc("TRN2", target_bir_lowering=False, num_devices=1)
    args = []
    for name, value in arrays.items():
        arrays[name] = value = np.ascontiguousarray(value)
        args.append(nc.dram_tensor(name, value.shape, mybir.dt.from_np(value.dtype), kind="ExternalInput").ap())
    args.append(nc.dram_tensor("out", (P, B, E), F32, kind="ExternalOutput").ap())
    build(nc, *args)
    r = run_bass_kernel_spmd(nc, [arrays], core_ids=[0])
    return r.results[0]["out"].transpose(1, 0, 2)
```

```python
from contextlib import ExitStack

import numpy as np

import concourse.bass as bass
from concourse import mybir
from concourse.alu_op_type import AluOpType as ALU

ACT = mybir.ActivationFunctionType
AX_X = mybir.AxisListType.X
F32 = mybir.dt.float32
F32R = mybir.dt.float32r
I32 = mybir.dt.int32

P = 128
B = 8
E = 512
C = E // P
T = B * P
NH = 32
G = 8
J = NH // G
HALF = T // 2
TPH = B // 2
MAX_POS = 512
PC = MAX_POS // P
THETA = 10000.0
NE = 16
NX = NE + 2
RG = 4
EPG = NE // RG
SCALE = 1.0 / float(np.sqrt(np.float32(P)))
MASKED = -1.0e9
HUGE = 3.0e38
EPS = 1e-5
OUT_OF_REACH = 1.0e30
MAGIC = float(0x5F3759DF)
BLOCK = 32
BLOCKS = 3 * BLOCK
HOTS_POOL = 3

EARLY, LATE = range(2)
HALF1 = [("K", 1, 0, 0, EARLY), ("Q", 1, 0, 0, LATE), ("Q", 1, 1, 1, EARLY), ("Q", 1, 2, 2, EARLY),
         ("Q", 1, 3, 2, LATE), ("VT", 1, 0, 3, EARLY), ("V", 1, 0, 4, EARLY)]
HALF0 = [("K", 0, 0, 4, LATE), ("Q", 0, 0, 5, EARLY), ("Q", 0, 1, 6, EARLY), ("Q", 0, 2, 7, EARLY),
         ("Q", 0, 3, 7, LATE), ("VT", 0, 0, 8, LATE), ("V", 0, 0, 9, LATE)]
NP0 = len(HALF0)
PROJECTIONS = HALF1 + HALF0
NP = len(PROJECTIONS)
STEPS = B + 2
PROLOGUE_Q = list(range(NP0 + 1, NP0 + 1 + J))
PROLOGUE_V = list(range(NP0 + 1 + J, NP))
STAGED = range(2 * TPH, 3 * TPH)
STATS_STEP, NORM_STEP, TURN_STEP, INNER_STEP = 5, 6, 7, 8
D2 = P // 2
WEIGHTS = ["k", "q0", "q1", "q2", "q3", "v"]
SPLIT_STEP = [1, 2, 3, 4, 5, 6]
NW = len(WEIGHTS)


def is_roped(p):
    return p[0] in ("Q", "K")


NR0 = sum(map(is_roped, HALF0))
NR = sum(map(is_roped, PROJECTIONS))


def weight_of(kind, j):
    return WEIGHTS.index({"Q": f"q{j}", "K": "k", "VT": "v"}[kind])


def made_before(g, n):
    return g * NP + NP0 + n


def roped_before(g, n):
    return g * NR + NR0 + sum(map(is_roped, PROJECTIONS[:n]))


def made_in(s, when, last):
    return [n for n in range(NP0 if last else NP) if PROJECTIONS[n][3:] == (s, when)]


def place(kind, h, j=0):
    return next(n for n, p in enumerate(PROJECTIONS) if p[:3] == (kind, h, j))


def build(nc, x, ctx_in, pos, mask, wq, wkv, wo, rw, rb, rbias, w12, w3, b3, rope, iota, ident_in, out):
    with ExitStack() as stack:
        def sb(name, shape, dt=F32):
            return stack.enter_context(nc.sbuf_tensor(f"sb_{name}", shape, dt))

        def sem(name):
            return stack.enter_context(nc.semaphore(f"s_{name}"))

        bank = [stack.enter_context(nc.psum_tensor(f"bank{i}_ps", [P, 512], F32)) for i in range(8)]

        acc = sb("acc", [P, B, E])
        act_hi = sb("act_hi", [P, C, T], F32R)
        act_lo = sb("act_lo", [P, C, T], F32R)
        ctx_hi = sb("ctx_hi", [P, C, T], F32R)
        ctx_lo = sb("ctx_lo", [P, C, T], F32R)
        cap = sb("cap", [P, B, P])
        cos_t = sb("cos_t", [P, T])
        sin_t = sb("sin_t", [P, T])
        q_t = sb("q_t", [P, J, T])
        k_t = sb("k_t", [P, T])
        v_t = sb("v_t", [P, HALF])
        v_hi = sb("v_hi", [P, B, P], F32R)
        v_lo = sb("v_lo", [P, B, P], F32R)
        wq_raw = sb("wq_raw", [P, J, C, P])
        wq_hi = sb("wq_hi", [P, J, C, P], F32R)
        wq_lo = sb("wq_lo", [P, J, C, P], F32R)
        wkv_raw = sb("wkv_raw", [P, 2, C, P])
        wkv_hi = sb("wkv_hi", [P, 2, C, P], F32R)
        wkv_lo = sb("wkv_lo", [P, 2, C, P], F32R)
        wo_raw = sb("wo_raw", [P, J, E])
        wo_hi = sb("wo_hi", [P, J, E], F32R)
        wo_lo = sb("wo_lo", [P, J, E], F32R)
        capped = sb("capped", [P, 2, J, P])
        probs = sb("probs", [P, 2, J, P])
        probs_hi = sb("probs_hi", [P, J * P], F32R)
        probs_lo = sb("probs_lo", [P, J * P], F32R)
        o_hi = sb("o_hi", [P, J, P], F32R)
        o_lo = sb("o_lo", [P, J, P], F32R)
        rope_a = sb("rope_a", [P, 2, HALF])
        rope_b = sb("rope_b", [P, 2, HALF])
        neg_max = sb("neg_max", [P, 2, J])
        row_sum = sb("row_sum", [P, 2, J])
        row_inv = sb("row_inv", [P, 2, J])
        ident = sb("ident", [P, P])
        iota_t = sb("iota_t", [P, PC])
        stats = sb("stats", [P, B, 6])
        mean_var = sb("mean_var", [P, B, 2])
        var_eps = sb("var_eps", [P, B])
        minus_half = sb("minus_half", [P, B])
        rstd = sb("rstd", [P, B])
        tmp8 = sb("tmp8", [P, B])
        rw_hi = sb("rw_hi", [P, C, NE], F32R)
        rw_lo = sb("rw_lo", [P, C, NE], F32R)

        def normed(b):
            return q_t[:, b % TPH, b // TPH * HALF:(b // TPH + 1) * HALF]

        ctx_raw = q_t[:, :, HALF:T]
        ctx_raw2 = wo_raw
        rope_tab = v_t[:, :].rearrange("p (c n) -> p c n", n=P)
        one_hot = [v[:, tiles, :].rearrange("p b d -> p (b d)") for v in (v_hi, v_lo) for tiles in (slice(0, TPH), slice(TPH, B))]
        pos_f = rope_a[:, :, :].rearrange("p a t -> p (a t)")
        pos_i = capped[:, :, :, :].rearrange("p a j n -> p (a j n)").bitcast(I32)
        mask_i = rope_b[:, :, :].rearrange("p a (b k) -> p (a b) k", k=P).bitcast(I32)
        r1, r2, r3, r4 = (probs[:, i // 2, 2 * (i % 2), :].rearrange("p (b e) -> p b e", e=NE) for i in range(4))
        after = wkv_raw[:, :, :, :].rearrange("p a c n -> p (a c n)")
        rw_sb = after[:, 0:C * NE].rearrange("p (c e) -> p c e", c=C)
        rb_sb = after[:, 64:64 + NE]
        rbias_sb = after[:, 96:96 + NE]
        gates = after[:, 256:256 + B * NX].rearrange("p (b e) -> p b e", b=B)
        firsts = after[:, 112:112 + NE]
        earlier = after[:, 128:128 + RG * RG].rearrange("p (i k) -> p i k", i=RG)
        s8 = after[:, 400:400 + B]
        gmax = after[:, 416:416 + B * RG].rearrange("p (b g) -> p b g", b=B)
        keep = after[:, 448:448 + B * RG].rearrange("p (b g) -> p b g", b=B)
        silu_t = rope_a
        h_t = rope_b
        h_hi = ctx_hi[:, 0:2, 0:HALF]
        h_lo = ctx_lo[:, 0:2, 0:HALF]
        logits_t = cos_t[0:NE, :]
        gates_t = v_hi[0:BLOCKS, :, :].rearrange("p b d -> p (b d)")
        b3_raw = v_t[0:BLOCKS, :]
        b3_split = o_hi[0:BLOCKS, :, :].rearrange("p j t -> p (j t)")
        ew_raw, ew_hi, ew_lo = wq_raw, wq_hi, wq_lo
        ew3_both = wo_raw[:, :, :].rearrange("p j e -> p (j e)")
        tab_hi, tab_lo = (w[:, 1, :, :] for w in (wkv_hi, wkv_lo))
        staging = [t[:, i, :, :].rearrange("p j n -> p (j n)") for t in (probs, capped) for i in range(2)]
        beats = r2.rearrange("p b (i k) -> p b i k", i=RG)
        ties = r3.rearrange("p b (i k) -> p b i k", i=RG)

        x_loaded = [sem(f"x_loaded{h}") for h in range(2)]
        ctx_loaded = [sem(f"ctx_loaded{h}") for h in range(2)]
        pos_loaded = sem("pos_loaded")
        mask_loaded = sem("mask_loaded")
        consts_loaded = sem("consts_loaded")
        rope_loaded = sem("rope_loaded")
        router_loaded = sem("router_loaded")
        wq0_loaded = sem("wq0_loaded")
        wqkv_loaded = sem("wqkv_loaded")
        wo_loaded = sem("wo_loaded")
        cast_done = sem("cast_done")
        chain = sem("chain")
        normed_ready = sem("normed_ready")
        turned = sem("turned")
        turned_hi = sem("turned_hi")
        turned_split = sem("turned_split")
        tab_hi_done = sem("tab_hi_done")
        tab_split = sem("tab_split")
        pool_hot_ready = sem("pool_hot_ready")
        hot_ready = sem("hot_ready")
        hot_used = sem("hot_used")
        b3_cleared = sem("b3_cleared")
        b3_loaded = sem("b3_loaded")
        b3_hi_done = sem("b3_hi_done")
        b3_split_done = sem("b3_split_done")
        trig_ready = sem("trig_ready")
        wqkv_hi = sem("wqkv_hi")
        wqkv_split = sem("wqkv_split")
        wo_hi_done = sem("wo_hi_done")
        wo_split = sem("wo_split")
        proj_ready = sem("proj_ready")
        proj_read = sem("proj_read")
        proj_hi = sem("proj_hi")
        roped = sem("roped")
        scores_ready = sem("scores_ready")
        scores_capped = sem("scores_capped")
        max_ready = sem("max_ready")
        exp_done = sem("exp_done")
        inv_ready = sem("inv_ready")
        probs_ready = sem("probs_ready")
        probs_turned = sem("probs_turned")
        probs_hi_done = sem("probs_hi_done")
        probs_split = sem("probs_split")
        o_ready = sem("o_ready")
        o_hi_done = sem("o_hi_done")
        o_split = sem("o_split")
        out_ready = sem("out_ready")
        out_added = sem("out_added")
        stats_ready = sem("stats_ready")
        logits_ready = sem("logits_ready")
        logits_copied = sem("logits_copied")
        logits_turned = sem("logits_turned")
        logits_read = sem("logits_read")
        route_max = sem("route_max")
        route_exp = sem("route_exp")
        gates_ready = sem("gates_ready")
        gates_turned = sem("gates_turned")
        gates_hi_done = sem("gates_hi_done")
        gates_split = sem("gates_split")
        rw_split = sem("rw_split")
        staged = sem("staged")
        staged_split = sem("staged_split")
        rstd_ready = sem("rstd_ready")
        pool_chain = sem("pool_chain")
        order_ready = sem("order_ready")
        ew0_loaded = sem("ew0_loaded")
        ew30_loaded = sem("ew30_loaded")
        ew_loaded = sem("ew_loaded")
        ew3_loaded = sem("ew3_loaded")
        ew_hi_done = sem("ew_hi_done")
        ew_split = sem("ew_split")
        ew3_hi_done = sem("ew3_hi_done")
        ew3_split = sem("ew3_split")
        h1_ready = sem("h1_ready")
        h2_ready = sem("h2_ready")
        silu_done = sem("silu_done")
        h_done = sem("h_done")
        h_hi_done = sem("h_hi_done")
        h_split = sem("h_split")
        y_ready = sem("y_ready")
        y_added = sem("y_added")
        stored = sem("stored")

        def half(h):
            return slice(h * HALF, (h + 1) * HALF)

        def tile_cols(b):
            return slice(b * P, (b + 1) * P)

        def turn_bank(n):
            if n < 2 * B:
                return bank[4 + n % 4]
            return bank[(0, 1, 2, 3, 0, 1, 4, 5)[n - 2 * B]]

        def split_before(n):
            return n if n < STAGED[0] else n - len(STAGED)

        def ew_slot(e):
            return 2 if isinstance(e, int) and e == 1 else 0

        def ew3_raw(e):
            first = (E + 2) * at_start(e, 1)
            return ew3_both[:, first:first + E + 2]

        def ew3_half(w, e):
            return w[:, int(at_start(e, 1)), :, :].rearrange("p c n -> p (c n)")

        def inner_bank(e, h, a):
            swapped = at_start(e, 0) and h == 1 or at_start(e, 1) and h == 0
            return bank[2 * (1 - h if swapped else h) + a]

        def inner_before(e, h):
            if at_start(e, 0) and h == 1:
                return 2
            if at_start(e, 1) and h == 0:
                return 1
            return e * 2 + h

        def invert_std(engine, link, h):
            cols = slice(h * TPH, (h + 1) * TPH)
            y, v, m, t = rstd[:, cols], var_eps[:, cols], minus_half[:, cols], tmp8[:, cols]
            link(engine.tensor_scalar(v, mean_var[:, cols, 1], EPS, None, ALU.add))
            link(engine.tensor_scalar(y.bitcast(I32), v.bitcast(I32), -0.5, MAGIC, ALU.mult, ALU.add))
            link(engine.tensor_scalar(m, v, -0.5, None, ALU.mult))
            for i in range(3):
                link(engine.tensor_tensor(t, y, y, ALU.mult))
                link(engine.tensor_tensor(t, t, m, ALU.mult))
                if engine is nc.vector:
                    ins = engine.scalar_tensor_tensor(out=y, in0=t, scalar=1.5, in1=y, op0=ALU.add, op1=ALU.mult)
                else:
                    link(engine.tensor_scalar(t, t, 1.5, None, ALU.add))
                    ins = engine.tensor_tensor(y, y, t, ALU.mult)
                if i < 2:
                    link(ins)
            ins.then_inc(rstd_ready, 1)

        def hot(engine, n):
            return engine.tensor_scalar(one_hot[n % len(one_hot)], pos_f[:, half(n // PC)],
                                        iota_t[:, n % PC:n % PC + 1], None, ALU.is_equal)

        def at_start(g, n):
            return isinstance(g, int) and g == n

        def in_step(s):
            return s < B, 1 <= s <= B, 2 <= s <= B + 1

        block = stack.enter_context(nc.Block())

        @block.sync
        def _(sp):
            halves = [slice(0, TPH), slice(TPH, B)]
            sp.dma_start(acc[:, halves[0], :], x[:, halves[0], :]).then_inc(x_loaded[0], 16)
            sp.dma_start(pos_i, pos).then_inc(pos_loaded, 16)
            sp.dma_start(iota_t[:], iota).then_inc(pos_loaded, 16)
            sp.dma_start(rope_tab, rope).then_inc(rope_loaded, 16)
            sp.dma_start(ident[:], ident_in).then_inc(consts_loaded, 16)
            sp.dma_start(ctx_raw, ctx_in[:, halves[0], :]).then_inc(ctx_loaded[0], 16)
            sp.dma_start(wkv_raw[:], wkv[0]).then_inc(wqkv_loaded, 16)
            sp.dma_start(wq_raw[:], wq[0]).then_inc(wq0_loaded, 16)
            sp.dma_start(mask_i, mask).then_inc(mask_loaded, 16)
            sp.dma_start(acc[:, halves[1], :], x[:, halves[1], :]).then_inc(x_loaded[1], 16)
            sp.dma_start(ctx_raw2[:], ctx_in[:, halves[1], :]).then_inc(ctx_loaded[1], 16)
            sp.wait_ge(turned, 3 * TPH)
            sp.dma_start(wo_raw[:], wo[0]).then_inc(wo_loaded, 16)
            with sp.Fori(1, G) as g:
                sp.wait_ge(wqkv_split, g * NW)
                sp.dma_start(wq_raw[:], wq[bass.ds(g, 1)].rearrange("a p j c n -> p (a j) c n")).then_inc(wqkv_loaded, 16)
                sp.dma_start(wkv_raw[:], wkv[bass.ds(g, 1)].rearrange("a p j c n -> p (a j) c n")).then_inc(wqkv_loaded, 16)
                sp.wait_ge(wo_split, g * J)
                sp.dma_start(wo_raw[:], wo[bass.ds(g, 1)].rearrange("a p j n -> p (a j) n")).then_inc(wo_loaded, 16)
            sp.wait_ge(wqkv_split, G * NW)
            sp.dma_start(rw_sb, rw).then_inc(router_loaded, 16)
            sp.dma_start(rb_sb, rb).then_inc(router_loaded, 16)
            sp.dma_start(rbias_sb, rbias).then_inc(router_loaded, 16)
            for e in range(2):
                sp.dma_start(ew_raw[:, ew_slot(e):ew_slot(e) + 2], w12[e]).then_inc((ew0_loaded, ew_loaded)[e], 16)
            sp.wait_ge(wo_split, G * J)
            for e in range(2):
                sp.dma_start(ew3_raw(e), w3[e]).then_inc((ew30_loaded, ew3_loaded)[e], 16)
            sp.wait_ge(b3_cleared, 1)
            for i in range(3):
                sp.dma_start(b3_raw[i * BLOCK:i * BLOCK + NE + 1, :], b3).then_inc(b3_loaded, 16)
            with sp.Fori(2, NX) as e:
                sp.wait_ge(ew_split, e * 2)
                sp.dma_start(ew_raw[:, 0:2], w12[bass.ds(e, 1)].rearrange("a p j c n -> p (a j) c n")).then_inc(ew_loaded, 16)
                sp.wait_ge(ew3_split, e)
                sp.wait_ge(h_done, e * 2)
                sp.dma_start(ew3_raw(e), w3[bass.ds(e, 1)].rearrange("a p n -> p (a n)")).then_inc(ew3_loaded, 16)
            for b in range(B):
                sp.wait_ge(y_added, (NX - 1) * B + b + 1)
                sp.dma_start(out[:, b, :], acc[:, b, :]).then_inc(stored, 16)
            sp.wait_ge(stored, B * 16)

        @block.tensor
        def _(pe):
            def product(out_ap, st_hi, st_lo, mv_hi, mv_lo, first, last):
                pe.matmul(out_ap, st_lo, mv_hi, start=first, stop=False)
                pe.matmul(out_ap, st_hi, mv_lo, start=False, stop=False)
                return pe.matmul(out_ap, st_hi, mv_hi, start=False, stop=last)

            def project(n, g):
                kind, h, j = PROJECTIONS[n][:3]
                of = g + 1 - h
                dst = bank[(NP0 + n) % 2]
                if not (isinstance(g, int) and made_before(g, n) < 2):
                    pe.wait_ge(proj_read, made_before(g, n) - 1)
                if kind == "V":
                    pe.wait_ge(proj_read, made_before(g, place("VT", h)) + 1)
                    for i in range(TPH):
                        ins = pe.transpose(dst[:, tile_cols(i)], v_t[:, tile_cols(i)], ident[:, :])
                    ins.then_inc(proj_ready, 1)
                    return
                if h == 0:
                    pe.wait_ge(wqkv_split, of * NW + weight_of(kind, j) + 1)
                elif at_start(g, 0) and kind == "K":
                    pe.wait_ge(staged_split, len(STAGED))
                elif at_start(g, 0) and kind == "Q" and j == 0:
                    pe.wait_ge(turned_split, split_before(2 * B))
                w_hi, w_lo = (wq_hi, wq_lo) if kind == "Q" else (wkv_hi, wkv_lo)
                slot = {"Q": j, "K": 0, "VT": 1}[kind]
                m_hi, m_lo = (act_hi, act_lo) if kind == "Q" else (ctx_hi, ctx_lo)
                for c in range(C):
                    ins = product(dst[:, :], w_hi[:, slot, c, :], w_lo[:, slot, c, :],
                                  m_hi[:, c, half(h)], m_lo[:, c, half(h)], c == 0, c == C - 1)
                ins.then_inc(proj_ready, 1)

            def turn_tile(src, n):
                if n == 2 * B + TPH - 1:
                    pe.wait_ge(scores_capped, G * B)
                if n - 2 * B in (4, 5):
                    pe.wait_ge(h_done, 1)
                if n - 2 * B in (6, 7):
                    pe.wait_ge(y_added, n - 2 * B - 5)
                earlier_tile = n - TPH
                if n in range(TPH, 2 * B):
                    if earlier_tile in STAGED:
                        pe.wait_ge(staged, earlier_tile - STAGED[0] + 1)
                    else:
                        pe.wait_ge(turned_split, split_before(earlier_tile) + 1)
                for c in range(C):
                    ins = pe.transpose(turn_bank(n)[:, tile_cols(c)], src[:, c * P:(c + 1) * P], ident[:, :])
                ins.then_inc(turned, 1)

            def expert_inner(e, h, a):
                if a == 0:
                    if h == 0:
                        pe.wait_ge(ew_split, e * 2 + 2)
                    if at_start(e, 0) and h == 1:
                        pe.wait_ge(h_done, 1)
                    elif not (isinstance(e, int) and e < 2 and h == 0):
                        pe.wait_ge(h_done, e * 2 + h - 1)
                for c in range(C):
                    ins = product(inner_bank(e, h, a)[:, :], ew_hi[:, ew_slot(e) + a, c, :], ew_lo[:, ew_slot(e) + a, c, :],
                                  act_hi[:, c, half(h)], act_lo[:, c, half(h)], c == 0, c == C - 1)
                ins.then_inc((h1_ready, h2_ready)[a], 1)

            def expert_out(e, b, biases=False):
                if b == 0:
                    pe.wait_ge(ew3_split, e + 1)
                if b % TPH == 0:
                    pe.wait_ge(h_split, inner_before(e, b // TPH) + 1)
                if not (at_start(e, 0) and b < 4):
                    pe.wait_ge(y_added, e * B + b - 3)
                dst = bank[4 + b % 4][:, :]
                if biases:
                    pe.matmul(dst, gates_t[:, tile_cols(b)], b3_split, start=True, stop=False)
                product(dst, h_hi[:, b // TPH, tile_cols(b % TPH)], h_lo[:, b // TPH, tile_cols(b % TPH)],
                        ew3_half(wkv_hi, e), ew3_half(wkv_lo, e), not biases, True).then_inc(y_ready, 1)

            def router(h):
                for c in range(C):
                    ins = product(bank[2 + h][0:NE, :], rw_hi[:, c, :], rw_lo[:, c, :], act_hi[:, c, half(h)],
                                  act_lo[:, c, half(h)], c == 0, c == C - 1)
                ins.then_inc(logits_ready, 1)

            def turn_logits():
                pe.wait_ge(logits_copied, 2)
                for b in range(B):
                    ins = pe.transpose(bank[2][:, b * NE:(b + 1) * NE], logits_t[:, tile_cols(b)], ident[0:NE, 0:NE])
                ins.then_inc(logits_turned, 1)

            def attend(g, last):
                for s in range(STEPS):
                    a, t, w = in_step(s)
                    if a:
                        if s in (0, TPH):
                            pe.wait_ge(roped, roped_before(g, 0 if s == 0 else NP0))
                        if not (isinstance(g, int) and g == 0 and s < 2):
                            pe.wait_ge(scores_capped, g * B + s - 1)
                        for j in range(J):
                            ins = pe.matmul(bank[2 + s % 2][:, tile_cols(j)], q_t[:, j, tile_cols(s)],
                                            k_t[:, tile_cols(s)], start=True, stop=True)
                        ins.then_inc(scores_ready, 1)
                    if t:
                        b = s - 1
                        pe.wait_ge(probs_ready, g * B + b + 1)
                        for j in range(J):
                            ins = pe.transpose(bank[4][:, tile_cols(j)], probs[:, b % 2, j, :], ident[:, :])
                        ins.then_inc(probs_turned, 1)
                    for n in made_in(s, EARLY, last):
                        project(n, g)
                    if w:
                        b = s - 2
                        pe.wait_ge(o_split, g * B + b + 1)
                        if b == 0:
                            pe.wait_ge(wo_split, g * J + J)
                        if not (isinstance(g, int) and g == 0 and b < 2):
                            pe.wait_ge(out_added, g * B + b - 1)
                        for j in range(J):
                            ins = product(bank[6 + b % 2][:, :], o_hi[:, j, :], o_lo[:, j, :],
                                          wo_hi[:, j, :], wo_lo[:, j, :], j == 0, j == J - 1)
                        ins.then_inc(out_ready, 1)
                    if t:
                        b = s - 1
                        if b in (0, TPH):
                            pe.wait_ge(proj_read, made_before(g, 0 if b == 0 else NP0))
                        pe.wait_ge(probs_split, g * B + b + 1)
                        product(bank[5][:, :], v_hi[:, b, :], v_lo[:, b, :], probs_hi[:, :], probs_lo[:, :],
                                True, True).then_inc(o_ready, 1)
                    for n in made_in(s, LATE, last):
                        project(n, g)
                    if last and s == TURN_STEP:
                        for b in range(TPH):
                            pe.wait_ge(normed_ready, B + b + 1)
                            turn_tile(normed(b), 2 * B + b)
                    if last and s == INNER_STEP:
                        pe.wait_ge(turned_split, split_before(2 * B + TPH))
                        expert_inner(0, 0, 0)

            def cos_sin(h):
                for c in range(PC):
                    n = h * PC + c
                    if n < HOTS_POOL:
                        pe.wait_ge(pool_hot_ready, n + 1)
                    else:
                        pe.wait_ge(hot_ready, n + 1 - HOTS_POOL)
                    pe.matmul(bank[2 + h][:, :], tab_lo[:, c, :], one_hot[n % 4], start=(c == 0), stop=False)
                    pe.matmul(bank[2 + h][:, :], tab_hi[:, c, :], one_hot[n % 4],
                              start=False, stop=(c == PC - 1)).then_inc(hot_used, 1)

            pe.wait_ge(consts_loaded, 16)
            pe.wait_ge(ctx_loaded[0], 16)
            for b in range(TPH):
                turn_tile(ctx_raw[:, b, :], b)
            for b in range(TPH):
                pe.wait_ge(normed_ready, b + 1)
                turn_tile(normed(b), TPH + b)
            pe.wait_ge(tab_split, 1)
            cos_sin(0)
            pe.wait_ge(turned_split, TPH)
            project(NP0, -1)
            pe.wait_ge(turned_split, 2 * TPH)
            project(PROLOGUE_Q[0], -1)
            cos_sin(1)
            pe.wait_ge(ctx_loaded[1], 16)
            for b in range(TPH):
                turn_tile(ctx_raw2[:, b, :], STAGED[b])
            for n in PROLOGUE_Q[1:] + PROLOGUE_V[:1]:
                project(n, -1)
            for b in range(TPH):
                pe.wait_ge(normed_ready, TPH + b + 1)
                turn_tile(normed(TPH + b), 3 * TPH + b)
            project(PROLOGUE_V[1], -1)
            pe.wait_ge(trig_ready, 8)
            attend(0, False)
            with pe.Fori(1, G - 1) as g:
                attend(g, False)
            attend(G - 1, True)

            expert_inner(0, 0, 1)
            expert_inner(1, 0, 0)
            pe.wait_ge(out_added, G * B - 1)
            for b in range(TPH):
                if b == 3:
                    pe.wait_ge(out_added, G * B)
                expert_out(0, b)
            for b in range(TPH, B):
                pe.wait_ge(normed_ready, B + b + 1)
                turn_tile(normed(b), 2 * B + b)
            expert_inner(1, 0, 1)
            pe.wait_ge(turned_split, split_before(3 * B))
            for a in range(2):
                expert_inner(0, 1, a)
            pe.wait_ge(rw_split, 1)
            pe.wait_ge(h_done, 2)
            router(0)
            router(1)
            for b in range(TPH, B):
                expert_out(0, b)
                if b == TPH + 1:
                    turn_logits()
            pe.wait_ge(logits_read, 1)
            for a in range(2):
                expert_inner(1, 1, a)
            for b in range(TPH):
                expert_out(1, b)
            for a in range(2):
                expert_inner(2, 0, a)
            expert_inner(2, 1, 0)
            for b in range(TPH, B):
                expert_out(1, b)
            pe.wait_ge(gates_ready, 1)
            pe.wait_ge(h_done, inner_before(2, 0) + 1)
            for i in range(B):
                ins = pe.transpose(bank[i // TPH][0:NE + 1, tile_cols(i % TPH)], gates[:, i, 1:NX], ident[:, :])
            ins.then_inc(gates_turned, 1)
            expert_inner(2, 1, 1)
            for b in range(B):
                expert_out(2, b)
            pe.wait_ge(gates_split, 2)

            def expert(e, biases=False):
                for h in range(2):
                    for a in range(2):
                        expert_inner(e, h, a)
                for b in range(B):
                    expert_out(e, b, biases)

            with pe.Fori(3, NX - 1) as e:
                expert(e)
            pe.wait_ge(b3_split_done, 1)
            expert(NX - 1, True)

        @block.scalar
        def _(act):
            def turn_hi(n, dst):
                act.wait_ge(turned, n + 1)
                nc.scalar.copy(dst, turn_bank(n)[:, :].rearrange("p (c t) -> p c t", c=C)).then_inc(turned_hi, 1)

            def split_qkv(i, g):
                w = WEIGHTS[i]
                if w[0] == "q":
                    src, dst = wq_raw[:, int(w[1])], wq_hi[:, int(w[1])]
                else:
                    src, dst = wkv_raw[:, "kv".index(w)], wkv_hi[:, "kv".index(w)]
                if isinstance(g, int) and g == 0:
                    if i == 0:
                        act.wait_ge(wqkv_loaded, 16)
                    if WEIGHTS[i] == "v":
                        act.wait_ge(hot_used, 2 * PC)
                    if i == 1:
                        act.wait_ge(wq0_loaded, 16)
                else:
                    if i == 0:
                        act.wait_ge(wqkv_loaded, g * 32 + 16)
                    kind = {"q": "Q", "k": "K", "v": "VT"}[w[0]]
                    act.wait_ge(proj_ready, made_before(g - 1, place(kind, 1, int(w[1]) if w[0] == "q" else 0)) + 1)
                nc.scalar.copy(dst, src).then_inc(wqkv_hi, 1)

            def split_wo(j, g):
                if j == 0:
                    act.wait_ge(wo_loaded, g * 16 + 16)
                    if not (isinstance(g, int) and g == 0):
                        act.wait_ge(out_ready, g * B)
                nc.scalar.copy(wo_hi[:, j, :], wo_raw[:, j, :]).then_inc(wo_hi_done, 1)

            def project_hi(n, g):
                kind, h, j = PROJECTIONS[n][:3]
                if kind == "V":
                    act.wait_ge(proj_ready, made_before(g, n) + 1)
                    nc.scalar.copy(v_hi[:, h * TPH:(h + 1) * TPH, :],
                                   bank[(NP0 + n) % 2][:, :].rearrange("p (b d) -> p b d", d=P)).then_inc(proj_hi, 1)

            def expert_w(e):
                if at_start(e, 0):
                    act.wait_ge(ew0_loaded, 16)
                else:
                    act.wait_ge(ew_loaded, e * 16)
                if isinstance(e, int) and e < 2:
                    act.wait_ge(proj_ready, G * NP)
                elif at_start(e, 2):
                    act.wait_ge(h2_ready, inner_before(0, 1) + 1)
                else:
                    act.wait_ge(h2_ready, e * 2)
                for a in range(ew_slot(e), ew_slot(e) + 2):
                    nc.scalar.copy(ew_hi[:, a], ew_raw[:, a]).then_inc(ew_hi_done, 1)

            def expert_w3(e):
                if at_start(e, 0):
                    act.wait_ge(ew30_loaded, 16)
                else:
                    act.wait_ge(ew3_loaded, e * 16)
                if at_start(e, 2):
                    act.wait_ge(y_ready, B)
                elif not (isinstance(e, int) and e < 2):
                    act.wait_ge(y_ready, e * B)
                nc.scalar.copy(ew3_half(wkv_hi, e), ew3_raw(e)[:, 0:E]).then_inc(ew3_hi_done, 1)

            def expert_inner(e, h):
                n = inner_before(e, h)
                act.wait_ge(h1_ready, n + 1)
                nc.scalar.activation(silu_t[:, h, :], inner_bank(e, h, 0)[:, :], ACT.Silu,
                                     bias=ew3_raw(e)[:, E:E + 1], scale=1.0).then_inc(silu_done, 1)
                act.wait_ge(h_done, n + 1)
                if isinstance(e, int) and e in (1, 2) and h == 0:
                    act.wait_ge(y_ready, (e - 1) * B + TPH)
                nc.scalar.copy(h_hi[:, h, :], h_t[:, h, :]).then_inc(h_hi_done, 1)

            def logits_out(h):
                act.wait_ge(logits_ready, h + 1)
                nc.scalar.copy(logits_t[:, half(h)], bank[2 + h][0:NE, :]).then_inc(logits_copied, 1)

            def attend(g, last, first=False):
                for s in range(STEPS):
                    a, t, w = in_step(s)
                    if t:
                        act.wait_ge(probs_turned, g * B + s)
                        nc.scalar.copy(probs_hi[:, :], bank[4][:, :]).then_inc(probs_hi_done, 1)
                    if last and s == TURN_STEP + 1:
                        for b in range(TPH):
                            turn_hi(2 * B + b, act_hi[:, :, tile_cols(b)])
                    if a:
                        act.wait_ge(max_ready, g * B + s + 1)
                        for j in range(J):
                            ins = nc.scalar.activation(probs[:, s % 2, j, :], capped[:, s % 2, j, :], ACT.Exp,
                                                       bias=neg_max[:, s % 2, j:j + 1], scale=1.0,
                                                       accum_out=row_sum[:, s % 2, j:j + 1])
                        ins.then_inc(exp_done, 1)
                    for n in made_in(s, EARLY, last):
                        project_hi(n, g)
                    if t:
                        act.wait_ge(o_ready, g * B + s)
                        nc.scalar.copy(o_hi[:, :, :], bank[5][:, :].rearrange("p (j t) -> p j t", j=J)).then_inc(o_hi_done, 1)
                    if not last:
                        for i in range(NW):
                            if SPLIT_STEP[i] == s:
                                split_qkv(i, g + 1)
                    if s == 0 and not first:
                        for j in range(J):
                            split_wo(j, g)
                    for n in made_in(s, LATE, last):
                        project_hi(n, g)
                    if last and s in (4, 5):
                        expert_w(s - 4)
                    if last and s in (6, 7):
                        expert_w3(s - 6)

            def cos_sin(h):
                act.wait_ge(hot_used, (h + 1) * PC)
                nc.scalar.copy(cos_t[0:D2, half(h)], bank[2 + h][0:D2, :]).then_inc(trig_ready, 1)
                nc.scalar.copy(cos_t[D2:P, half(h)], bank[2 + h][0:D2, :]).then_inc(trig_ready, 1)
                nc.scalar.copy(sin_t[0:D2, half(h)], bank[2 + h][D2:P, :]).then_inc(trig_ready, 1)
                nc.scalar.mul(sin_t[D2:P, half(h)], bank[2 + h][D2:P, :], -1.0).then_inc(trig_ready, 1)

            act.wait_ge(rope_loaded, 16)
            nc.scalar.copy(tab_hi, rope_tab).then_inc(tab_hi_done, 1)
            for b in range(TPH):
                turn_hi(b, ctx_hi[:, :, tile_cols(b)])
                if b == 2:
                    split_qkv(0, 0)
            for b in range(TPH):
                turn_hi(TPH + b, act_hi[:, :, tile_cols(b)])
            split_qkv(1, 0)
            cos_sin(0)
            for i in range(2, NW - 1):
                split_qkv(i, 0)
            cos_sin(1)
            split_qkv(NW - 1, 0)
            for i, n in enumerate(STAGED):
                turn_hi(n, ctx_hi[:, :, tile_cols(TPH + i)])
                if i == 2:
                    act.wait_ge(cast_done, 1)
                nc.scalar.copy(staging[i], turn_bank(n)[:, :]).then_inc(staged, 1)
            for b in range(TPH):
                turn_hi(3 * TPH + b, act_hi[:, :, tile_cols(TPH + b)])
            project_hi(NP - 1, -1)
            for j in range(J):
                split_wo(j, 0)
            attend(0, False, True)
            with act.Fori(1, G - 1) as g:
                attend(g, False)
            attend(G - 1, True)

            expert_inner(0, 0)
            for b in range(TPH, B):
                turn_hi(2 * B + b, act_hi[:, :, tile_cols(b)])
            expert_inner(1, 0)
            expert_inner(0, 1)
            logits_out(0)
            logits_out(1)
            act.wait_ge(route_max, 1)
            nc.scalar.activation(r2, r1, ACT.Exp).then_inc(route_exp, 1)
            expert_w(2)
            expert_inner(1, 1)
            expert_w3(2)
            expert_inner(2, 0)
            act.wait_ge(b3_loaded, 48)
            nc.scalar.copy(b3_split, b3_raw).then_inc(b3_hi_done, 1)
            act.wait_ge(gates_turned, 1)
            for h in range(2):
                for first in (0, 2 * BLOCK):
                    nc.scalar.copy(gates_t[first:first + NE + 1, half(h)], bank[h][0:NE + 1, :]).then_inc(gates_hi_done, 1)
            expert_inner(2, 1)
            expert_w(3)

            def expert(e):
                expert_w3(e)
                for h in range(2):
                    expert_inner(e, h)

            with act.Fori(3, NX - 1) as e:
                expert(e)
                expert_w(e + 1)
            expert(NX - 1)

        @block.gpsimd
        def _(pool):
            def low(dst, raw, hi):
                return nc.gpsimd.tensor_tensor(dst, raw, hi.bitcast(F32), ALU.subtract)

            count = [0]

            def link(ins):
                count[0] += 1
                ins.then_inc(pool_chain, 1)
                pool.wait_ge(pool_chain, count[0])

            def split_qkv(i, g):
                w = WEIGHTS[i]
                pool.wait_ge(wqkv_hi, g * NW + i + 1)
                if w[0] == "q":
                    j = int(w[1])
                    ins = low(wq_lo[:, j], wq_raw[:, j], wq_hi[:, j])
                else:
                    a = "kv".index(w)
                    ins = low(wkv_lo[:, a], wkv_raw[:, a], wkv_hi[:, a])
                ins.then_inc(wqkv_split, 1)

            def split_wo(j, g):
                pool.wait_ge(wo_hi_done, g * J + j + 1)
                low(wo_lo[:, j, :], wo_raw[:, j, :], wo_hi[:, j, :]).then_inc(wo_split, 1)

            def rotate(n, g):
                kind, h, j = PROJECTIONS[n][:3]
                if not is_roped(PROJECTIONS[n]):
                    return
                part = roped_before(0, n) % 2
                pool.wait_ge(proj_read, made_before(g, n) + 1)
                dst = q_t[:, j, half(h)] if kind == "Q" else k_t[:, half(h)]
                nc.gpsimd.tensor_tensor(dst, rope_a[:, part, :], rope_b[:, part, :], ALU.add).then_inc(roped, 1)

            def attend(g, last, first=False):
                for s in range(STEPS):
                    if s > 0:
                        for n in made_in(s - 1, LATE, last):
                            rotate(n, g)
                    if s == 0 and not first:
                        for j in range(J):
                            split_wo(j, g)
                    if not last:
                        for i in range(NW):
                            if SPLIT_STEP[i] == s:
                                split_qkv(i, g + 1)
                    for n in made_in(s, EARLY, last):
                        rotate(n, g)
                    if last and s in (5, 6):
                        expert_w(s - 5)
                    if last and s == STATS_STEP:
                        pool.wait_ge(stats_ready, 2 * (B + TPH))
                        invert_std(nc.gpsimd, link, 0)
                    if last and s in (7, 8):
                        expert_w3(s - 7)

            def expert_w(e):
                for a in range(2):
                    pool.wait_ge(ew_hi_done, e * 2 + a + 1)
                    b = ew_slot(e) + a
                    low(ew_lo[:, b], ew_raw[:, b], ew_hi[:, b]).then_inc(ew_split, 1)

            def expert_w3(e):
                pool.wait_ge(ew3_hi_done, e + 1)
                low(ew3_half(wkv_lo, e), ew3_raw(e)[:, 0:E], ew3_half(wkv_hi, e)).then_inc(ew3_split, 1)

            pool.wait_ge(tab_hi_done, 1)
            low(tab_lo, rope_tab, tab_hi).then_inc(tab_split, 1)
            pool.wait_ge(cast_done, 1)
            for n in range(HOTS_POOL):
                hot(nc.gpsimd, n).then_inc(pool_hot_ready, 1)
            for i in range(3):
                split_qkv(i, 0)
            rotate(NP0, -1)
            for i in range(3, 5):
                split_qkv(i, 0)
            rotate(PROLOGUE_Q[0], -1)
            split_qkv(5, 0)
            for i, n in enumerate(STAGED):
                pool.wait_ge(staged, i + 1)
                low(ctx_lo[:, :, tile_cols(TPH + i)], staging[i].rearrange("p (c t) -> p c t", c=C),
                    ctx_hi[:, :, tile_cols(TPH + i)]).then_inc(staged_split, 1)
                if i < 3:
                    rotate(PROLOGUE_Q[1 + i], -1)
            for j in range(J):
                split_wo(j, 0)
            attend(0, False, True)
            with pool.Fori(1, G - 1) as g:
                attend(g, False)
            attend(G - 1, True)

            pool.wait_ge(proj_ready, G * NP)
            nc.gpsimd.memset(b3_raw, 0.0).then_inc(b3_cleared, 1)
            pool.wait_ge(o_ready, G * B)
            nc.gpsimd.memset(gates_t.bitcast(F32), 0.0).then_inc(order_ready, 1)
            pool.wait_ge(router_loaded, 48)
            nc.gpsimd.memset(gates[:, :, :], 1.0).then_inc(order_ready, 1)
            for e in range(NE):
                nc.gpsimd.memset(firsts[:, e:e + 1], float(NE - e)).then_inc(order_ready, 1)
            for i in range(RG):
                for k in range(RG):
                    nc.gpsimd.memset(earlier[:, i, k:k + 1], float(k < i)).then_inc(order_ready, 1)
            pool.wait_ge(stats_ready, 4 * B)
            invert_std(nc.gpsimd, link, 1)
            with pool.Fori(2, NX) as e:
                expert_w(e)
                expert_w3(e)

        @block.vector
        def _(dve):
            count = [0]

            def link(ins):
                count[0] += 1
                ins.then_inc(chain, 1)
                dve.wait_ge(chain, count[0])

            def tile_stats(b, done):
                nc.vector.bn_stats(stats[:, b, :], acc[:, b, :]).then_inc(stats_ready, 1)
                dve.wait_ge(stats_ready, 2 * done + 1)
                nc.vector.bn_aggr(mean_var[:, b, :], stats[:, b, :]).then_inc(stats_ready, 1)

            def normalise(h, n):
                dve.wait_ge(rstd_ready, n)
                for b in range(h * TPH, (h + 1) * TPH):
                    nc.vector.tensor_scalar(normed(b), acc[:, b, :], mean_var[:, b, 0:1], rstd[:, b:b + 1],
                                            ALU.subtract, ALU.mult).then_inc(normed_ready, 1)

            def turn_lo(n, hi, lo):
                dve.wait_ge(turned_hi, n + 1)
                nc.vector.tensor_tensor(lo, turn_bank(n)[:, :].rearrange("p (c t) -> p c t", c=C), hi.bitcast(F32),
                                        ALU.subtract).then_inc(turned_split, 1)

            def project_out(n, g):
                kind, h, j = PROJECTIONS[n][:3]
                dve.wait_ge(proj_ready, made_before(g, n) + 1)
                src = bank[(NP0 + n) % 2]
                if kind == "VT":
                    nc.vector.tensor_copy(v_t[:, :], src[:, :]).then_inc(proj_read, 1)
                elif kind == "V":
                    dve.wait_ge(proj_hi, g * 2 + 3 - h)
                    tiles = slice(h * TPH, (h + 1) * TPH)
                    nc.vector.tensor_tensor(v_lo[:, tiles, :], src[:, :].rearrange("p (b d) -> p b d", d=P),
                                            v_hi[:, tiles, :].bitcast(F32), ALU.subtract).then_inc(proj_read, 1)
                else:
                    r = roped_before(0, n) % 2
                    if not (isinstance(g, int) and roped_before(g, n) < 2):
                        dve.wait_ge(roped, roped_before(g, n) - 1)
                    nc.vector.tensor_tensor(rope_a[:, r, :], src[:, :], cos_t[:, half(h)], ALU.mult)
                    nc.vector.tensor_tensor(rope_b[D2:P, r, :], src[0:D2, :], sin_t[0:D2, half(h)], ALU.mult)
                    nc.vector.tensor_tensor(rope_b[0:D2, r, :], src[D2:P, :], sin_t[D2:P, half(h)],
                                            ALU.mult).then_inc(proj_read, 1)

            def attend(g, last):
                for s in range(STEPS):
                    a, t, w = in_step(s)
                    if a:
                        dve.wait_ge(scores_ready, g * B + s + 1)
                        nc.vector.scalar_tensor_tensor(
                            out=capped[:, s % 2, :, :], in0=bank[2 + s % 2][:, :].rearrange("p (j k) -> p j k", j=J),
                            scalar=SCALE, in1=cap[:, s:s + 1, :].to_broadcast([P, J, P]), op0=ALU.mult,
                            op1=ALU.min).then_inc(scores_capped, 1)
                        dve.wait_ge(scores_capped, g * B + s + 1)
                        nc.vector.tensor_reduce(neg_max[:, s % 2, :], capped[:, s % 2, :, :], AX_X, ALU.max,
                                                negate=True).then_inc(max_ready, 1)
                    if t:
                        dve.wait_ge(probs_hi_done, g * B + s)
                        nc.vector.tensor_tensor(probs_lo[:, :], bank[4][:, :], probs_hi[:, :].bitcast(F32),
                                                ALU.subtract).then_inc(probs_split, 1)
                    if s > 0:
                        for n in made_in(s - 1, LATE, last):
                            project_out(n, g)
                    if last and s == TURN_STEP + 1:
                        for b in range(TPH):
                            turn_lo(2 * B + b, act_hi[:, :, tile_cols(b)], act_lo[:, :, tile_cols(b)])
                    if a:
                        dve.wait_ge(exp_done, g * B + s + 1)
                        nc.vector.reciprocal(row_inv[:, s % 2, :], row_sum[:, s % 2, :]).then_inc(inv_ready, 1)
                        dve.wait_ge(inv_ready, g * B + s + 1)
                        nc.vector.tensor_tensor(probs[:, s % 2, :, :], probs[:, s % 2, :, :],
                                                row_inv[:, s % 2, :].unsqueeze(2).to_broadcast([P, J, P]),
                                                ALU.mult).then_inc(probs_ready, 1)
                    for n in made_in(s, EARLY, last):
                        project_out(n, g)
                    if w:
                        b = s - 2
                        dve.wait_ge(out_ready, g * B + b + 1)
                        nc.vector.tensor_tensor(acc[:, b, :], acc[:, b, :], bank[6 + b % 2][:, :],
                                                ALU.add).then_inc(out_added, 1)
                    if t:
                        dve.wait_ge(o_hi_done, g * B + s)
                        nc.vector.tensor_tensor(o_lo[:, :, :], bank[5][:, :].rearrange("p (j t) -> p j t", j=J),
                                                o_hi[:, :, :].bitcast(F32), ALU.subtract).then_inc(o_split, 1)
                    if last and w:
                        dve.wait_ge(out_added, g * B + s - 1)
                        tile_stats(s - 2, B + s - 2)
                    if s == STEPS - 1:
                        for n in made_in(s, LATE, last):
                            project_out(n, g)
                    if last and s == NORM_STEP:
                        normalise(0, 3)

            def expert_inner(e, h, first_tile=False):
                n = inner_before(e, h)
                dve.wait_ge(h2_ready, n + 1)
                dve.wait_ge(silu_done, n + 1)
                nc.vector.scalar_tensor_tensor(out=h_t[:, h, :], in0=inner_bank(e, h, 1)[:, :],
                                               scalar=ew3_raw(e)[:, E + 1:E + 2], in1=silu_t[:, h, :],
                                               op0=ALU.add, op1=ALU.mult).then_inc(h_done, 1)
                if h == 1 and first_tile:
                    expert_added(e, [0])
                dve.wait_ge(h_hi_done, n + 1)
                nc.vector.tensor_tensor(h_lo[:, h, :], h_t[:, h, :], h_hi[:, h, :].bitcast(F32),
                                        ALU.subtract).then_inc(h_split, 1)

            def expert_added(e, tiles):
                for b in tiles:
                    dve.wait_ge(y_ready, e * B + b + 1)
                    nc.vector.scalar_tensor_tensor(out=acc[:, b, :], in0=bank[4 + b % 4][:, :],
                                                   scalar=gates[:, b, bass.ds(e, 1)], in1=acc[:, b, :],
                                                   op0=ALU.mult, op1=ALU.add).then_inc(y_added, 1)

            dve.wait_ge(x_loaded[0], 16)
            for b in range(TPH):
                tile_stats(b, b)
            dve.wait_ge(pos_loaded, 32)
            nc.vector.tensor_copy(pos_f, pos_i).then_inc(cast_done, 1)
            dve.wait_ge(stats_ready, 2 * TPH)
            invert_std(nc.vector, link, 0)
            normalise(0, 1)
            dve.wait_ge(cast_done, 1)
            for n in range(HOTS_POOL, PC):
                hot(nc.vector, n).then_inc(hot_ready, 1)
            for b in range(TPH):
                turn_lo(b, ctx_hi[:, :, tile_cols(b)], ctx_lo[:, :, tile_cols(b)])
            for b in range(TPH):
                turn_lo(TPH + b, act_hi[:, :, tile_cols(b)], act_lo[:, :, tile_cols(b)])
            dve.wait_ge(hot_used, PC)
            for n in range(PC, 2 * PC):
                hot(nc.vector, n).then_inc(hot_ready, 1)
            dve.wait_ge(hot_ready, 2 * PC - HOTS_POOL)
            dve.wait_ge(mask_loaded, 16)
            nc.vector.tensor_scalar(cap[:, :, :], mask_i, 0.0, -HUGE, ALU.is_equal, ALU.mult).then_inc(cast_done, 1)
            dve.wait_ge(trig_ready, 4)
            dve.wait_ge(cast_done, 2)
            project_out(NP0, -1)
            nc.vector.tensor_scalar(cap[:, :, :], cap[:, :, :], HUGE, MASKED, ALU.add, ALU.add).then_inc(cast_done, 1)
            dve.wait_ge(x_loaded[1], 16)
            for b in range(TPH, B):
                tile_stats(b, b)
            project_out(PROLOGUE_Q[0], -1)
            dve.wait_ge(stats_ready, 2 * B)
            invert_std(nc.vector, link, 1)
            for n in PROLOGUE_Q[1:]:
                project_out(n, -1)
            normalise(1, 2)
            project_out(PROLOGUE_V[0], -1)
            for b in range(TPH):
                turn_lo(3 * TPH + b, act_hi[:, :, tile_cols(TPH + b)], act_lo[:, :, tile_cols(TPH + b)])
            project_out(PROLOGUE_V[1], -1)
            dve.wait_ge(trig_ready, 8)
            dve.wait_ge(cast_done, 3)
            attend(0, False)
            with dve.Fori(1, G - 1) as g:
                attend(g, False)
            attend(G - 1, True)

            dve.wait_ge(router_loaded, 48)
            link(nc.vector.tensor_copy(rw_hi[:, :, :], rw_sb))
            nc.vector.tensor_tensor(rw_lo[:, :, :], rw_sb, rw_hi[:, :, :].bitcast(F32),
                                    ALU.subtract).then_inc(rw_split, 1)
            expert_inner(0, 0)
            normalise(1, 4)
            dve.wait_ge(order_ready, 2)
            expert_added(0, range(TPH))
            for b in range(TPH, B):
                turn_lo(2 * B + b, act_hi[:, :, tile_cols(b)], act_lo[:, :, tile_cols(b)])
            expert_inner(1, 0)
            expert_inner(0, 1)
            def over(ap, n):
                return ap.unsqueeze(2).to_broadcast([P, B, n])

            dve.wait_ge(logits_turned, 1)
            logits = bank[2][:, 0:B * NE].rearrange("p (b e) -> p b e", e=NE)
            bias_b = rb_sb.unsqueeze(1).to_broadcast([P, B, NE])
            nc.vector.tensor_tensor(r3, logits, bias_b, ALU.add).then_inc(logits_read, 1)
            dve.wait_ge(logits_read, 1)
            link(nc.vector.tensor_reduce(s8, r3, AX_X, ALU.max))
            nc.vector.tensor_tensor(r1, r3, over(s8[:, :], NE), ALU.subtract).then_inc(route_max, 1)
            dve.wait_ge(route_exp, 1)
            link(nc.vector.reduce_sum(s8, r2, AX_X))
            link(nc.vector.reciprocal(tmp8[:], s8))
            link(nc.vector.tensor_tensor(r1, r2, over(tmp8[:, :], NE), ALU.mult))
            link(nc.vector.tensor_tensor(r1, r1, rbias_sb.unsqueeze(1).to_broadcast([P, B, NE]), ALU.add))
            link(nc.vector.tensor_reduce(gmax, r1.rearrange("p b (g e) -> p b g e", e=EPG), AX_X, ALU.max))
            dve.wait_ge(order_ready, 2 + NE + RG * RG)
            of_k = gmax.unsqueeze(2).to_broadcast([P, B, RG, RG])
            of_i = gmax.unsqueeze(3).to_broadcast([P, B, RG, RG])
            link(nc.vector.tensor_tensor(ties, of_k, of_i, ALU.is_equal))
            link(nc.vector.tensor_tensor(ties, ties, earlier.unsqueeze(1).to_broadcast([P, B, RG, RG]), ALU.mult))
            link(nc.vector.tensor_tensor(beats, of_k, of_i, ALU.is_gt))
            link(nc.vector.tensor_tensor(beats, beats, ties, ALU.add))
            link(nc.vector.reduce_sum(keep, beats, AX_X))
            link(nc.vector.tensor_scalar(keep, keep, 1.5, None, ALU.is_lt))
            expert_added(0, range(TPH, B))
            expert_inner(1, 1)
            keep_e = keep[:, :, :].unsqueeze(3).to_broadcast([P, B, RG, EPG])

            def v4_of(r):
                return r.rearrange("p b (g e) -> p b g e", e=EPG)

            link(nc.vector.tensor_scalar(keep, keep, 1.0, OUT_OF_REACH, ALU.subtract, ALU.mult))
            link(nc.vector.tensor_tensor(v4_of(r3), v4_of(r1), keep_e, ALU.add))
            for k in range(2):
                link(nc.vector.tensor_reduce(s8, r3, AX_X, ALU.max))
                link(nc.vector.tensor_tensor(r2, r3, over(s8[:, :], NE), ALU.is_equal))
                link(nc.vector.tensor_tensor(r2, r2, firsts[:, :].unsqueeze(1).to_broadcast([P, B, NE]), ALU.mult))
                link(nc.vector.tensor_reduce(s8, r2, AX_X, ALU.max))
                link(nc.vector.tensor_tensor(r2, r2, over(s8[:, :], NE), ALU.is_equal))
                if k == 0:
                    link(nc.vector.tensor_copy(r4, r2))
                    link(nc.vector.scalar_tensor_tensor(out=r3, in0=r2, scalar=-HUGE, in1=r3, op0=ALU.mult, op1=ALU.add))
                else:
                    link(nc.vector.tensor_tensor(r4, r4, r2, ALU.add))
            nc.vector.tensor_tensor(gates[:, :, 1:NE + 1], r1, r4, ALU.mult).then_inc(gates_ready, 1)

            dve.wait_ge(gates_ready, 1)
            expert_added(1, range(TPH))
            expert_inner(2, 0)
            expert_added(1, range(TPH, B))
            expert_inner(2, 1, True)
            expert_added(2, range(1, TPH))
            for h in range(2):
                dve.wait_ge(gates_hi_done, 2 * h + 2)
                nc.vector.tensor_tensor(gates_t[BLOCK:BLOCK + NE + 1, half(h)], bank[h][0:NE + 1, :],
                                        gates_t[0:NE + 1, half(h)].bitcast(F32), ALU.subtract).then_inc(gates_split, 1)
            expert_added(2, range(TPH, B))
            dve.wait_ge(b3_hi_done, 1)
            nc.vector.tensor_tensor(b3_split[2 * BLOCK:BLOCKS], b3_raw[2 * BLOCK:BLOCKS],
                                    b3_split[2 * BLOCK:BLOCKS].bitcast(F32), ALU.subtract).then_inc(b3_split_done, 1)
            with dve.Fori(3, NX) as e:
                expert_inner(e, 0)
                expert_inner(e, 1, True)
                expert_added(e, range(1, B))


def _rope_table():
    inv = (np.float32(1.0) / np.power(np.float32(THETA), np.arange(0, P, 2, dtype=np.float32) / np.float32(P))).astype(np.float32)
    f = np.arange(MAX_POS, dtype=np.float32)[:, None] * inv[None, :]
    tab = np.concatenate([np.cos(f), np.sin(f)], 1).astype(np.float32)
    return np.ascontiguousarray(tab.reshape(PC, P, P).transpose(1, 0, 2))


def kernel(x, ctx_4096, pos_BxS2, mask_BxSxS2_ik0, L0_xattn_Wq, L0_xattn_Wk, L0_xattn_Wv, L0_xattn_Wo,
           L0_ffn_router_w, L0_ffn_router_b, L0_ffn_router_bias, L0_ffn_ew1, L0_ffn_eb1, L0_ffn_ew2, L0_ffn_eb2,
           L0_ffn_ew3, L0_ffn_eb3, L0_ffn_sw1, L0_ffn_sb1, L0_ffn_sw2, L0_ffn_sb2, L0_ffn_sw3, L0_ffn_sb3):
    import concourse.bacc as bacc
    from concourse.bass_utils import run_bass_kernel_spmd

    a = np.asarray

    def around(routed, shared):
        return np.concatenate([shared[:1], routed, shared[1:]])

    def by_expert(routed, shared):
        both = around(a(routed), a(shared).reshape(E, 2, P).transpose(1, 0, 2))
        return both.reshape(NX, C, P, P).transpose(0, 2, 1, 3)

    wk, wv = (a(w).reshape(C, P, G, P).transpose(2, 1, 0, 3) for w in (L0_xattn_Wk, L0_xattn_Wv))
    arrays = {
        "x": a(x).transpose(1, 0, 2),
        "ctx_in": a(ctx_4096).transpose(1, 0, 2),
        "pos": np.broadcast_to(a(pos_BxS2).reshape(1, T), (P, T)),
        "mask": a(mask_BxSxS2_ik0).transpose(1, 0, 2),
        "wq": a(L0_xattn_Wq).reshape(C, P, G, J, P).transpose(2, 1, 3, 0, 4),
        "wkv": np.stack([wk, wv], 2),
        "wo": a(L0_xattn_Wo).reshape(G, J, P, E).transpose(0, 2, 1, 3),
        "rw": a(L0_ffn_router_w).reshape(C, P, NE).transpose(1, 0, 2),
        "rb": np.broadcast_to(a(L0_ffn_router_b), (P, NE)),
        "rbias": np.broadcast_to(a(L0_ffn_router_bias), (P, NE)),
        "w12": np.stack([by_expert(L0_ffn_ew1, L0_ffn_sw1), by_expert(L0_ffn_ew2, L0_ffn_sw2)], 2),
        "w3": around(
            np.concatenate([a(L0_ffn_ew3), a(L0_ffn_eb1)[:, :, None], a(L0_ffn_eb2)[:, :, None]], 2),
            np.concatenate([a(L0_ffn_sw3).reshape(2, P, E), a(L0_ffn_sb1).reshape(2, P, 1), a(L0_ffn_sb2).reshape(2, P, 1)], 2),
        ),
        "b3": np.concatenate([a(L0_ffn_eb3), a(L0_ffn_sb3).reshape(1, E)]),
        "rope": _rope_table(),
        "iota": (np.arange(P)[:, None] + P * np.arange(PC)[None, :]).astype(np.float32),
        "ident": np.eye(P, dtype=np.float32),
    }
    nc = bacc.Bacc("TRN2", target_bir_lowering=False, num_devices=1)
    args = []
    for name, value in arrays.items():
        arrays[name] = value = np.ascontiguousarray(value)
        args.append(nc.dram_tensor(name, value.shape, mybir.dt.from_np(value.dtype), kind="ExternalInput").ap())
    args.append(nc.dram_tensor("out", (P, B, E), F32, kind="ExternalOutput").ap())
    build(nc, *args)
    r = run_bass_kernel_spmd(nc, [arrays], core_ids=[0])
    return r.results[0]["out"].transpose(1, 0, 2)
```
